# Optimizing a Trainium2 kernel written in Bass

```python
import numpy as np
import jax
import jax.numpy as jnp

def _softmax(x, axis=-1):
    return jax.nn.softmax(x, axis=axis)

def _gelu(x):
    return jax.nn.gelu(x, approximate=True)

def _silu(x):
    return jax.nn.silu(x)

def _sigmoid(x):
    return jax.nn.sigmoid(x)

def _layernorm(x, axis=-1, eps=1e-05):
    m = jnp.mean(x, axis=axis, keepdims=True)
    v = jnp.var(x, axis=axis, keepdims=True)
    return (x - m) / jnp.sqrt(v + eps)

def _scatter_add(tgt, idx, src, axis=0):
    return tgt.at[idx].add(src)

def _segment_sum(src, seg, n):
    return jax.ops.segment_sum(src, seg, n)
kernel_name = 'mk_flamingo_gated_d1_seqx_r8_03339c'

def setup_inputs(seed: int=0):
    np.random.seed(seed)
    _w = jnp.asarray

    def _rec_inputs():
        import jax
        import jax.numpy as jnp
        _rk = jax.random.key(seed)
        x = -0.0003929 + 0.9999 * jax.random.normal(jax.random.fold_in(_rk, 1), (4, 256, 128), jnp.float32)
        _lenS = 256 - jax.random.randint(jax.random.fold_in(_rk, 7), (4,), 0, max(1, 256 // 4) + 1, jnp.int32)
        _lenS2 = 512 - jax.random.randint(jax.random.fold_in(_rk, 8), (4,), 0, max(1, 512 // 4) + 1, jnp.int32)
        _ctx_768P = jax.random.normal(jax.random.fold_in(_rk, 11), (4, 16, 96), jnp.float32)
        _ctx_768c = jax.random.dirichlet(jax.random.fold_in(_rk, 511), 0.3 * jnp.ones((16,), jnp.float32), (4, 512))
        _ctx_768t = jnp.einsum('bsk,bkd->bsd', _ctx_768c, _ctx_768P)
        _ctx_768t = _ctx_768t * jax.lax.rsqrt(jnp.mean(jnp.square(_ctx_768t)) + 1e-12) * 0.953939
        ctx_768 = -7.36909e-05 + 0.999899 * (_ctx_768t + 0.3 * jax.random.normal(jax.random.fold_in(_rk, 611), (4, 512, 96), jnp.float32))
        _g = jax.random.normal(jax.random.fold_in(_rk, 9001), (2, 1), jnp.float32)
        _g = jnp.sign(_g) * jnp.maximum(jnp.abs(_g), 1.0) + (_g == 0) * 1.0
        g_xattn = _g[0]
        g_ffn = _g[1]
        return (x, ctx_768, g_xattn, g_ffn)
    x, ctx_768, g_xattn, g_ffn = _rec_inputs()

    def _L0_xattn_setup():
        import jax, jax.numpy as jnp
        import numpy as np
        IMG_DIM, TXT_DIM, HID = (128, 96, 128)
        B, LQ, LK = (8, 256, 256)
        key = jax.random.key(seed)
        ks = jax.random.split(key, 8)
        s_img = 1.0 / np.sqrt(IMG_DIM)
        s_txt = 1.0 / np.sqrt(TXT_DIM)
        return {'image_features': jax.random.normal(ks[0], (B, LQ, IMG_DIM), jnp.float32), 'text_features': jax.random.normal(ks[1], (B, LK, TXT_DIM), jnp.float32), 'Wq': jax.random.uniform(ks[2], (IMG_DIM, HID), jnp.float32, -s_img, s_img), 'bq': jax.random.uniform(ks[3], (HID,), jnp.float32, -s_img, s_img), 'Wk': jax.random.uniform(ks[4], (TXT_DIM, HID), jnp.float32, -s_txt, s_txt), 'bk': jax.random.uniform(ks[5], (HID,), jnp.float32, -s_txt, s_txt), 'Wv': jax.random.uniform(ks[6], (TXT_DIM, HID), jnp.float32, -s_txt, s_txt), 'bv': jax.random.uniform(ks[7], (HID,), jnp.float32, -s_txt, s_txt)}
    _L0_xattn_all = _L0_xattn_setup()
    _L0_xattn_in = {k: v for k, v in _L0_xattn_all.items() if k in ('Wq', 'bq', 'Wk', 'bk', 'Wv', 'bv')}
    del _L0_xattn_all

    def _L0_ffn_setup():
        import jax, jax.numpy as jnp
        import numpy as np
        D_MODEL = 128
        N_HEADS = 16
        D_HEAD = D_MODEL // N_HEADS
        N_EXPERTS = 8
        TOP_K = 2
        D_FF = 256
        EPS = 1e-06

        def rmsnorm(x, w):
            return x * jax.lax.rsqrt(jnp.mean(x * x, axis=-1, keepdims=True) + EPS) * w

        def swiglu(x, w_gate, w_up, w_down):
            return jax.nn.silu(x @ w_gate) * (x @ w_up) @ w_down
        key = jax.random.key(seed)
        ks = jax.random.split(key, 16)
        s = 0.02
        B, S = (2, 256)
        return {'X': jax.random.normal(ks[0], (B, S, D_MODEL), dtype=jnp.float32), 'norm1_w': jnp.ones((D_MODEL,), jnp.float32), 'norm2_w': jnp.ones((D_MODEL,), jnp.float32), 'wq': jax.random.normal(ks[1], (D_MODEL, D_MODEL), jnp.float32) * s, 'wk': jax.random.normal(ks[2], (D_MODEL, D_MODEL), jnp.float32) * s, 'wv': jax.random.normal(ks[3], (D_MODEL, D_MODEL), jnp.float32) * s, 'wo': jax.random.normal(ks[4], (D_MODEL, D_MODEL), jnp.float32) * s, 'router_w': jax.random.normal(ks[5], (D_MODEL, N_EXPERTS), jnp.float32) * s, 'sh_gate': jax.random.normal(ks[6], (D_MODEL, D_FF), jnp.float32) * s, 'sh_up': jax.random.normal(ks[7], (D_MODEL, D_FF), jnp.float32) * s, 'sh_down': jax.random.normal(ks[8], (D_FF, D_MODEL), jnp.float32) * s, 'e_gate': jax.random.normal(ks[9], (N_EXPERTS, D_MODEL, D_FF), jnp.float32) * s, 'e_up': jax.random.normal(ks[10], (N_EXPERTS, D_MODEL, D_FF), jnp.float32) * s, 'e_down': jax.random.normal(ks[11], (N_EXPERTS, D_FF, D_MODEL), jnp.float32) * s}
    _L0_ffn_all = _L0_ffn_setup()
    _L0_ffn_in = {k: v for k, v in _L0_ffn_all.items() if k in ('norm1_w', 'norm2_w', 'wq', 'wk', 'wv', 'wo', 'router_w', 'sh_gate', 'sh_up', 'sh_down', 'e_gate', 'e_up', 'e_down')}
    del _L0_ffn_all
    return {'x': x, 'ctx_768': ctx_768, 'g_xattn': g_xattn, 'g_ffn': g_ffn, 'L0_xattn_Wq': _L0_xattn_in['Wq'], 'L0_xattn_bq': _L0_xattn_in['bq'], 'L0_xattn_Wk': _L0_xattn_in['Wk'], 'L0_xattn_bk': _L0_xattn_in['bk'], 'L0_xattn_Wv': _L0_xattn_in['Wv'], 'L0_xattn_bv': _L0_xattn_in['bv'], 'L0_ffn_norm1_w': _L0_ffn_in['norm1_w'], 'L0_ffn_norm2_w': _L0_ffn_in['norm2_w'], 'L0_ffn_wq': _L0_ffn_in['wq'], 'L0_ffn_wk': _L0_ffn_in['wk'], 'L0_ffn_wv': _L0_ffn_in['wv'], 'L0_ffn_wo': _L0_ffn_in['wo'], 'L0_ffn_router_w': _L0_ffn_in['router_w'], 'L0_ffn_sh_gate': _L0_ffn_in['sh_gate'], 'L0_ffn_sh_up': _L0_ffn_in['sh_up'], 'L0_ffn_sh_down': _L0_ffn_in['sh_down'], 'L0_ffn_e_gate': _L0_ffn_in['e_gate'], 'L0_ffn_e_up': _L0_ffn_in['e_up'], 'L0_ffn_e_down': _L0_ffn_in['e_down']}

def reference(x, ctx_768, g_xattn, g_ffn, L0_xattn_Wq, L0_xattn_bq, L0_xattn_Wk, L0_xattn_bk, L0_xattn_Wv, L0_xattn_bv, L0_ffn_norm1_w, L0_ffn_norm2_w, L0_ffn_wq, L0_ffn_wk, L0_ffn_wv, L0_ffn_wo, L0_ffn_router_w, L0_ffn_sh_gate, L0_ffn_sh_up, L0_ffn_sh_down, L0_ffn_e_gate, L0_ffn_e_up, L0_ffn_e_down):
    import jax
    import jax.numpy as jnp

    def _L0_xattn_ref(image_features, text_features, Wq, bq, Wk, bk, Wv, bv):
        import jax, jax.numpy as jnp
        import numpy as np
        IMG_DIM, TXT_DIM, HID = (128, 96, 128)
        B, LQ, LK = (8, 256, 256)
        query = jnp.einsum('bqi,ih->bqh', image_features, Wq) + bq
        key = jnp.einsum('bkt,th->bkh', text_features, Wk) + bk
        value = jnp.einsum('bkt,th->bkh', text_features, Wv) + bv
        scale = 1.0 / jnp.sqrt(jnp.asarray(HID, query.dtype))
        scores = jnp.einsum('bqh,bkh->bqk', query, key) * scale
        weights = jax.nn.softmax(scores, axis=-1)
        attended = jnp.einsum('bqk,bkh->bqh', weights, value)
        return attended

    def _L0_ffn_ref(X, norm1_w, norm2_w, wq, wk, wv, wo, router_w, sh_gate, sh_up, sh_down, e_gate, e_up, e_down):
        import jax, jax.numpy as jnp
        import numpy as np
        D_MODEL = 128
        N_HEADS = 16
        D_HEAD = D_MODEL // N_HEADS
        N_EXPERTS = 8
        TOP_K = 2
        D_FF = 256
        EPS = 1e-06

        def rmsnorm(x, w):
            return x * jax.lax.rsqrt(jnp.mean(x * x, axis=-1, keepdims=True) + EPS) * w

        def swiglu(x, w_gate, w_up, w_down):
            return jax.nn.silu(x @ w_gate) * (x @ w_up) @ w_down
        B, S, d = X.shape
        scale = 1.0 / jnp.sqrt(jnp.asarray(D_HEAD, X.dtype))
        h = rmsnorm(X, norm1_w)
        q = (h @ wq).reshape(B, S, N_HEADS, D_HEAD)
        k = (h @ wk).reshape(B, S, N_HEADS, D_HEAD)
        v = (h @ wv).reshape(B, S, N_HEADS, D_HEAD)
        scores = jnp.einsum('bshd,bthd->bhst', q, k) * scale
        attn = jax.nn.softmax(scores, axis=-1)
        ctx = jnp.einsum('bhst,bthd->bshd', attn, v).reshape(B, S, d)
        X = X + ctx @ wo
        h2 = rmsnorm(X, norm2_w).reshape(B * S, d)
        logits = h2 @ router_w
        probs = jax.nn.softmax(logits, axis=-1)
        topw, topi = jax.lax.top_k(probs, TOP_K)
        topw = jax.nn.softmax(topw, axis=-1)
        combine = jnp.sum(jax.nn.one_hot(topi, N_EXPERTS, dtype=h2.dtype) * topw[..., None], axis=1)
        shared = swiglu(h2, sh_gate, sh_up, sh_down)
        gate = jnp.einsum('td,edf->etf', h2, e_gate)
        up = jnp.einsum('td,edf->etf', h2, e_up)
        eout = jnp.einsum('etf,efd->etd', jax.nn.silu(gate) * up, e_down)
        spec = jnp.einsum('etd,te->td', eout, combine)
        moe_out = (shared + spec).reshape(B, S, d)
        return X + moe_out
    x = x + jnp.tanh(g_xattn[0]) * _L0_xattn_ref(_layernorm(x, axis=-1), ctx_768, L0_xattn_Wq, L0_xattn_bq, L0_xattn_Wk, L0_xattn_bk, L0_xattn_Wv, L0_xattn_bv)
    x = x + jnp.tanh(g_ffn[0]) * _L0_ffn_ref(_layernorm(x, axis=-1), L0_ffn_norm1_w, L0_ffn_norm2_w, L0_ffn_wq, L0_ffn_wk, L0_ffn_wv, L0_ffn_wo, L0_ffn_router_w, L0_ffn_sh_gate, L0_ffn_sh_up, L0_ffn_sh_down, L0_ffn_e_gate, L0_ffn_e_up, L0_ffn_e_down)
    return x

_drawn_inputs = setup_inputs


def setup_inputs(seed=0):
    import zlib

    import numpy as np

    out = dict(_drawn_inputs(seed))
    spreads = {'L0_ffn_norm1_w': (1.0, 0.6), 'L0_ffn_norm2_w': (1.0, 0.556)}
    factors = {'L0_xattn_bq': 8.0, 'L0_xattn_bk': 8.0, 'L0_ffn_wq': 8.0, 'L0_ffn_wk': 8.0}
    for name, (base, spread) in spreads.items():
        noise = np.random.default_rng([zlib.crc32(name.encode()), seed]).standard_normal(out[name].shape)
        drawn = base * np.exp(spread * noise) if base else spread * noise
        out[name] = jnp.asarray(drawn.astype(out[name].dtype))
    for name, factor in factors.items():
        out[name] = (out[name] * factor).astype(out[name].dtype)
    return out
```

```python
from contextlib import ExitStack

import concourse.bass as bass
from concourse import mybir

ALU = mybir.AluOpType
ACT = mybir.ActivationFunctionType
AX_X = mybir.AxisListType.X
F32 = mybir.dt.float32
F32R = mybir.dt.float32r

P = 128
LN_EPS = 1e-5
RMS_EPS = 1e-6
NSTACK = 3
LAG = 21
PV_LAG = LAG + 2
C_LAG = PV_LAG + 16
NSPLIT = 3
NRAW = 2


def bank_uses(pairs):
    place = {}
    for banks, uses in pairs:
        for n, use in enumerate(uses):
            place[use] = (banks[n % len(banks)], n // len(banks))
    return place


def flamingo_block(nc, x, ctx_768, g_xattn, g_ffn, xWq, xbq, xWk, xbk, xWv, xbv, norm1_w, norm2_w,
                   wq, wk, wv, wo, router_w, sh_gate, sh_up, sh_down, e_gate, e_up, e_down, out):
    NB, L, D = x.shape
    LK, DC = ctx_768.shape[1:]
    NE, _, FF = e_gate.shape
    NT = NB * L // P
    TB = L // P
    KC = LK // P
    DH = 8
    NH = D // DH
    NG = NH // 2
    NQ = NH // 4
    SCALE_X = float(D) ** -0.5
    SCALE_H = float(DH) ** -0.5
    NHEADS = NB * NH
    NEXP = NE + 1
    HALF = NB * L // 2

    scratch = nc.dram_tensor("split_scratch", [NB, 2, 2, 2, DH, NG, L], F32, kind="Internal").ap()

    SLOTS_X = NT + 6
    turn_uses = [("ctxT", 0), ("ctxT", 1), ("xnT", 0), ("ctxT", 2), ("xnT", 1), ("ctxT", 3), ("xnT", 2), ("xnT", 3)]
    proj_uses = [("k", 0), ("v", 0), ("k", 1), ("v", 1), ("q", 0), ("k", 2), ("v", 2), ("q", 1),
                 ("k", 3), ("v", 3), ("q", 2), ("q", 3)]
    for slot in range(SLOTS_X):
        if 0 <= slot - 2 < NT:
            turn_uses.append(("pT", slot - 2))
        if slot >= 6 and slot % 2 == 0 and (slot - 6) // 2 < NB:
            turn_uses.append(("hT", (slot - 6) // 2))
        if slot >= 7 and slot % 2 == 1 and (slot - 7) // 2 < NB:
            proj_uses += [("qk2", (slot - 7) // 2), ("v2", (slot - 7) // 2)]

    misc_at = {}
    for b in range(NB):
        misc_at.setdefault(16 * b + 17, []).append(("mT", b))
        base = 16 * b + C_LAG
        for off, step in ((0, "uT"), (2, "cT"), (4, "wo"), (7, "h2T"), (10, "router")):
            misc_at.setdefault(base + off, []).append((step, b))
        if b % 2:
            for off, step in ((11, "route_exp1"), (12, "route_top"), (13, "route_exp2"), (15, "route_weights")):
                misc_at.setdefault(base + off, []).append((step, b))
    SLOTS_A = max(misc_at) + 1
    misc_uses = []
    for slot in range(SLOTS_A):
        for step, b in misc_at.get(slot, []):
            if step == "uT":
                misc_uses += [("uT", b, 0), ("uT", b, 1)]
            elif not step.startswith("route_"):
                misc_uses.append((step, b))

    items = [(0, 0), (1, 0), (0, 1), (1, 1)] + [(e, h) for e in range(2, NEXP) for h in range(2)]
    NI = len(items)
    last_item_of = {e: max(n for n, it in enumerate(items) if it[0] == e) for e in range(NEXP)}

    place = bank_uses([
        ((0, 1), turn_uses + [("max", n) for n in range(NHEADS)] + [("gate", n, f) for n in range(NI) for f in range(2)]),
        ((2, 3), proj_uses + [("exp", n) for n in range(NHEADS)] + [("up", n, f) for n in range(NI) for f in range(2)]),
        ((4, 5), [("s", i) for i in range(NT)] + [("pv", n) for n in range(NHEADS // 4)] + [("down", n) for n in range(NI)]),
        ((6, 7), [("o", i) for i in range(NT)] + misc_uses),
    ])

    with ExitStack() as ctx:
        def sb(name, shape, dt=F32):
            return ctx.enter_context(nc.sbuf_tensor(name, shape, dt))

        def sem(name):
            return ctx.enter_context(nc.semaphore(name))

        banks = [ctx.enter_context(nc.psum_tensor(f"bank{i}", [P, 512], F32)) for i in range(8)]
        filled = [sem(f"filled{i}") for i in range(8)]
        emptied = [sem(f"emptied{i}") for i in range(8)]

        ident = sb("ident", [P, P])
        Wq_s, Wk_s, Wv_s = sb("Wq_s", [D, D]), sb("Wk_s", [DC, D]), sb("Wv_s", [DC, D])
        bq_s, bk_s = sb("bq_s", [D, 1]), sb("bk_s", [D, 1])
        bv_row = sb("bv_row", [P, D])
        gates = sb("gates", [P, 2])
        tg = sb("tg", [P, 2])
        n1_s, n2_s = sb("n1_s", [D, 1]), sb("n2_s", [D, 1])
        wqk_raw = sb("wqk_raw", [D, 2, D])
        wqk = sb("wqk", [D, 2, D])
        wv_s, wo_s = sb("wv_s", [D, D]), sb("wo_s", [D, D])
        router_s, router_pad = sb("router_s", [D, NE]), sb("router_pad", [D, P])

        xs = sb("xs", [P, NT, D])
        x1 = sb("x1", [P, NT, D])
        y = sb("y", [P, NT, D])
        ctx_s = sb("ctx_s", [P, NB * KC, DC])
        ctxT = sb("ctxT", [DC, NB, LK])
        kT = sb("kT", [D, NB, LK])
        vx = sb("vx", [P, NB * KC, D])
        qT = sb("qT", [D, NB, L])
        xnT = sb("xnT", [D, NB, L])
        probs = sb("probs", [P, 2, LK])
        probsT = sb("probsT", [P, 2, KC, P])
        bn6 = sb("bn6", [P, 2, NT, 6])
        mv = sb("mv", [P, 2, NT, 2])
        small = sb("small", [P, 12, NT])
        neg_half = sb("neg_half", [P, 2, TB])
        ms2 = sb("ms2", [P, NT])
        split = sb("split", [P, 2, 2, 2, L], F32R)
        vh = sb("vh", [P, NT, NH, 32])
        q_st = sb("q_st", [96, NSTACK, NG, L], F32R)
        k_st = sb("k_st", [96, NSTACK, NH, L], F32R)
        mxs = sb("mxs", [P, NB, TB, NH])
        negmT = sb("negmT", [NH, 2, L], F32R)
        ep = ctx_s[:].rearrange("p c d -> p (c d)").rearrange("p (n t s) -> p n t s", n=3, t=TB)
        u = probsT[:].rearrange("p n c t -> p (n c t)").rearrange("p (g s) -> p g s", g=NQ)
        rden = sb("rden", [P, TB, NH])
        cn = sb("cn", [P, TB, NH, DH])
        cT = sb("cT", [D, L])
        h2 = sb("h2", [P, TB, D])
        h2T = probs[:].rearrange("p n s -> p (n s)").rearrange("p (b s) -> p b s", b=NB)
        h2hi, h2lo = sb("h2hi", [D, NB * L], F32R), sb("h2lo", [D, NB * L], F32R)
        rt = sb("rt", [P, 12, NT, NE])
        rs = sb("rs", [P, 12, NT])
        widx = sb("widx", [P, NE])
        cw = sb("cw", [P, NT, NE])
        raw = sb("raw", [D, NRAW, 2, FF])
        whi, wlo = sb("whi", [D, NSPLIT, 2, FF], F32R), sb("wlo", [D, NSPLIT, 2, FF], F32R)
        down = sb("down", [P, NEXP, 2, D])
        silu = kT[:].rearrange("p b t -> p (b t)").rearrange("p (n f t) -> p n f t", n=2, f=2)
        act_t = vx[:].rearrange("p a d -> p (a d)").rearrange("p (n f t) -> p n f t", n=2, f=2)

        ld_x = [sem(f"ld_x{b}") for b in range(NB)]
        ld_ctx = [sem(f"ld_ctx{b}") for b in range(NB)]
        ld_kv, ld_q, ld_bv, ld_ffn, ld_down = sem("ld_kv"), sem("ld_q"), sem("ld_bv"), sem("ld_ffn"), sem("ld_down")
        ld_raw = [sem(f"ld_raw{e}") for e in range(NRAW)]
        scratch_written = [sem(f"scratch_written{b}") for b in range(NB)]
        stacked = [sem(f"stacked{b}") for b in range(NB)]
        m_placed = [sem(f"m_placed{b}") for b in range(NB)]
        out_stored = sem("out_stored")
        pool_step, dve_step = sem("pool_step"), sem("dve_step")
        ident_ready, tg_ready, xb_ready = sem("ident_ready"), sem("tg_ready"), sem("xb_ready")
        wqk_ready, router_ready, vh_ready, pads_ready = sem("wqk_ready"), sem("router_ready"), sem("vh_ready"), sem("pads_ready")
        m_rows_zero = sem("m_rows_zero")
        xn_ready, hs_ready, hi_ready = sem("xn_ready"), sem("hs_ready"), sem("hi_ready")
        nb_ready = sem("nb_ready")
        norm1_in, norm1_out, norm2_in, norm2_out, norm3_out = (
            sem("norm1_in"), sem("norm1_out"), sem("norm2_in"), sem("norm2_out"), sem("norm3_out"))
        ms2_ready, h2_ready, h2s_ready, w_split = sem("ms2_ready"), sem("h2_ready"), sem("h2s_ready"), sem("w_split")
        pv_heads, ld_gates, route_in, route_exp = sem("pv_heads"), sem("ld_gates"), sem("route_in"), sem("route_exp")

        def b_of(use):
            return banks[place[use][0]]

        def may_fill(eng, use):
            bank, before = place[use]
            if before:
                eng.wait_ge(emptied[bank], before)

        def full(use):
            return filled[place[use][0]]

        def is_full(eng, use):
            bank, before = place[use]
            eng.wait_ge(filled[bank], before + 1)

        def free(use):
            return emptied[place[use][0]]

        def is_read(eng, use):
            bank, before = place[use]
            eng.wait_ge(emptied[bank], before + 1)

        def pv_done(eng, n):
            if n % 4 == 3:
                is_full(eng, ("pv", n // 4))
            else:
                eng.wait_ge(pv_heads, 3 * (n // 4) + n % 4 + 1)

        block = ctx.enter_context(nc.Block())

        def load_raw(sp, e):
            gate_w, up_w = (sh_gate, sh_up) if e == 0 else (e_gate[e - 1], e_up[e - 1])
            sp.dma_start(raw[:, e % NRAW, 0, :], gate_w).then_inc(ld_raw[e % NRAW], 16)
            sp.dma_start(raw[:, e % NRAW, 1, :], up_w).then_inc(ld_raw[e % NRAW], 16)

        def stack(sp, b):
            s = b % NSTACK
            is_read(sp, ("qk2", b))
            for qk in range(2):
                for part in range(2):
                    sp.dma_start(scratch[b, qk, :, part].rearrange("p d g s -> p (d g) s"),
                                 split[:, b % 2, part, qk, :].bitcast(F32)).then_inc(scratch_written[b], 16)
            sp.wait_ge(scratch_written[b], 64)
            if b < NSTACK:
                sp.wait_ge(pads_ready, b + 1)
            else:
                sp.wait_ge(m_rows_zero, b - NSTACK + 1)
            for p in range(2):
                for a in range(2):
                    r = 32 * p + 16 * a
                    q_src = scratch[b, 0, p, a].rearrange("d g s -> d (g s)").unsqueeze(0).broadcast_to([2, DH, NG * L])
                    sp.dma_start(q_st[r:r + 16, s].rearrange("r g s -> r (g s)").bitcast(F32),
                                 q_src).then_inc(stacked[b], 16)
                    k_src = scratch[b, 1, p].rearrange("c d g s -> (c d) g s")
                    sp.dma_start(k_st[r:r + 16, s, p::2, :].bitcast(F32), k_src).then_inc(stacked[b], 16)

        def place_m(sp, b):
            is_read(sp, ("mT", b))
            is_read(sp, ("max", NH * (b + 1) - 1))
            src = negmT[:, b % 2, :].bitcast(F32).unsqueeze(1).broadcast_to([NH, NG, L])
            sp.dma_start(q_st[64:64 + NH, b % NSTACK, :, :].bitcast(F32), src).then_inc(m_placed[b], 16)

        @block.sync
        def _(sp):
            for b in range(NB):
                sp.dma_start(ctx_s[:, b * KC:(b + 1) * KC, :],
                             ctx_768[b].rearrange("(c p) d -> p c d", p=P)).then_inc(ld_ctx[b], 16)
                sp.dma_start(xs[:, b * TB:(b + 1) * TB, :],
                             x[b].rearrange("(c p) d -> p c d", p=P)).then_inc(ld_x[b], 16)
                if b == 0:
                    sp.dma_start(Wk_s[:], xWk).then_inc(ld_kv, 16)
                    sp.dma_start(Wv_s[:], xWv).then_inc(ld_kv, 16)
                    sp.dma_start(bk_s[:], xbk.rearrange("(d o) -> d o", o=1)).then_inc(ld_kv, 16)
                    sp.dma_start(Wq_s[:], xWq).then_inc(ld_q, 16)
                    sp.dma_start(bq_s[:], xbq.rearrange("(d o) -> d o", o=1)).then_inc(ld_q, 16)
            sp.dma_start(n1_s[:], norm1_w.rearrange("(d o) -> d o", o=1)).then_inc(ld_ffn, 16)
            sp.dma_start(n2_s[:], norm2_w.rearrange("(d o) -> d o", o=1)).then_inc(ld_ffn, 16)
            sp.dma_start(wqk_raw[:, 0, :], wq).then_inc(ld_ffn, 16)
            sp.dma_start(wqk_raw[:, 1, :], wk).then_inc(ld_ffn, 16)
            sp.dma_start(wv_s[:], wv).then_inc(ld_ffn, 16)
            sp.dma_start(wo_s[:], wo).then_inc(ld_ffn, 16)
            sp.dma_start(router_s[:], router_w).then_inc(ld_ffn, 16)
            for e in range(NRAW):
                load_raw(sp, e)
            sp.dma_start(down[:, 0], sh_down.rearrange("(f p) d -> p f d", p=P)).then_inc(ld_down, 16)
            for e in range(NE):
                sp.dma_start(down[:, e + 1], e_down[e].rearrange("(f p) d -> p f d", p=P)).then_inc(ld_down, 16)

            for b in range(3):
                stack(sp, b)
            place_m(sp, 0)
            place_m(sp, 1)
            stack(sp, 3)
            place_m(sp, 2)
            place_m(sp, 3)
            for e in range(NRAW, NEXP):
                sp.wait_ge(w_split, e - NRAW + 1)
                load_raw(sp, e)
            for h in range(2):
                is_read(sp, ("down", NI - 2 + h))
                sp.dma_start(out.rearrange("b (c p) d -> p (b c) d", p=P)[:, h * 4:h * 4 + 4, :],
                             x1[:, h * 4:h * 4 + 4, :]).then_inc(out_stored, 16)
            sp.wait_ge(out_stored, 32)

        @block.gpsimd
        def _(pool):
            done = [0]

            def step(ins):
                done[0] += 1
                ins.then_inc(pool_step, 1)
                pool.wait_ge(pool_step, done[0])

            step(nc.gpsimd.memset(ident[:], 0.0))
            nc.gpsimd.affine_select(out=ident[:], in_=ident[:], compare_op=ALU.not_equal, fill=1.0, base=0,
                                    pattern=[[-1, P]], channel_multiplier=1).then_inc(ident_ready, 1)
            step(nc.gpsimd.memset(neg_half[:], -0.5))
            nc.gpsimd.memset(router_pad[:], 0.0).then_inc(pool_step, 1)
            for i in range(NE):
                last = nc.gpsimd.memset(widx[:, i:i + 1], float(NE - i))
            last.then_inc(pool_step, 1)
            done[0] += 2
            pool.wait_ge(ident_ready, 1)

            def pads(s):
                step(nc.gpsimd.memset(k_st[:, s].bitcast(F32), 0.0))
                step(nc.gpsimd.memset(q_st[64:96, s].bitcast(F32), 0.0))
                pick = ident[64:64 + NH, 64:64 + NH].unsqueeze(2).broadcast_to([NH, NH, L])
                nc.gpsimd.tensor_copy(k_st[64:64 + NH, s, :, :], pick).then_inc(pads_ready, 1)
                pool.wait_ge(pads_ready, s + 1)

            pads(0)

            def norm1(b):
                ts = slice(b * TB, (b + 1) * TB)
                pool.wait_ge(norm1_in, b + 1)
                nc.gpsimd.tensor_tensor(small[:, 8, ts], small[:, 0, ts], neg_half[:, 0], ALU.pow).then_inc(norm1_out, 1)

            def norm2(b):
                ts = slice(b * TB, (b + 1) * TB)
                pool.wait_ge(norm2_in, b + 1)
                nc.gpsimd.tensor_tensor(small[:, 5:7, ts], small[:, 3:5, ts], neg_half[:], ALU.pow).then_inc(norm2_out, 1)

            def norm3(b):
                ts = slice(b * TB, (b + 1) * TB)
                pool.wait_ge(ms2_ready, TB * (b + 1))
                step(nc.gpsimd.tensor_scalar(small[:, 7, ts], ms2[:, ts], RMS_EPS, None, ALU.add))
                nc.gpsimd.tensor_tensor(small[:, 11, ts], small[:, 7, ts], neg_half[:, 0], ALU.pow).then_inc(norm3_out, 1)

            for b in range(NB):
                norm1(b)
            pool.wait_ge(ld_bv, 16)
            pool.wait_ge(tg_ready, 1)
            step(nc.gpsimd.tensor_scalar(bv_row[:], bv_row[:], tg[:, 0:1], None, ALU.mult))
            for b in range(NB):
                pool.wait_ge(ld_x[b], 16)
                pool.wait_ge(xn_ready, b + 1)
                xb = xs[:, b * TB:(b + 1) * TB, :]
                nc.gpsimd.tensor_tensor(xb, xb, bv_row[:].unsqueeze(1).broadcast_to([P, TB, D]),
                                        ALU.add).then_inc(xb_ready, 1)
            pool.wait_ge(ld_ffn, 16 * 7)
            for i in range(2):
                nc.gpsimd.tensor_copy(wqk[:, i, :].rearrange("k (p d g) -> k p d g", p=2, d=DH),
                                      wqk_raw[:, i, :].rearrange("k (g p d) -> k p d g", p=2, d=DH)
                                      ).then_inc(wqk_ready, 1)
            pool.wait_ge(pool_step, done[0])
            nc.gpsimd.tensor_copy(router_pad[:, 0:NE], router_s[:]).then_inc(router_ready, 1)
            step(nc.gpsimd.memset(vh[:, 0:4], 0.0))
            step(nc.gpsimd.memset(vh[:, 4:8], 0.0))
            nc.gpsimd.memset(vh[:, :, :, DH:DH + 1], 1.0).then_inc(vh_ready, 1)

            def split_weights(e):
                pool.wait_ge(ld_raw[e % NRAW], 32 * (e // NRAW + 1))
                if e >= NSPLIT:
                    is_full(pool, ("up", last_item_of[e - NSPLIT], 1))
                step(nc.gpsimd.tensor_copy(whi[:, e % NSPLIT], raw[:, e % NRAW]))
                nc.gpsimd.tensor_tensor(wlo[:, e % NSPLIT], raw[:, e % NRAW], whi[:, e % NSPLIT].bitcast(F32),
                                        ALU.subtract).then_inc(w_split, 1)

            pads(1)
            norm2(0)
            split_weights(0)
            norm2(1)
            pads(2)
            norm2(2)
            split_weights(1)
            norm2(3)

            def split_h2(b):
                is_read(pool, ("h2T", b))
                step(nc.gpsimd.tensor_copy(h2hi[:, b * L:(b + 1) * L], h2T[:, b, :]))
                nc.gpsimd.tensor_tensor(h2lo[:, b * L:(b + 1) * L], h2T[:, b, :],
                                        h2hi[:, b * L:(b + 1) * L].bitcast(F32), ALU.subtract).then_inc(h2s_ready, 1)

            for b in range(NB - NSTACK):
                is_read(pool, ("exp", NH * (b + 1) - 1))
                nc.gpsimd.memset(q_st[64:96, b % NSTACK].bitcast(F32), 0.0).then_inc(m_rows_zero, 1)
                pool.wait_ge(m_rows_zero, b + 1)
            for b in range(NB):
                norm3(b)
                split_h2(b)
            for e in range(NRAW, NEXP):
                split_weights(e)

        @block.scalar
        def _(act):
            act.dma_start(bv_row[:], xbv.partition_broadcast(P)).then_inc(ld_bv, 16)
            act.dma_start(gates[:, 0:1], g_xattn.partition_broadcast(P)).then_inc(ld_gates, 16)
            act.dma_start(gates[:, 1:2], g_ffn.partition_broadcast(P)).then_inc(ld_gates, 16)
            act.wait_ge(ld_gates, 32)
            nc.scalar.activation(tg[:], gates[:], ACT.Tanh).then_inc(tg_ready, 1)

            def ctx_turn(b):
                is_full(act, ("ctxT", b))
                nc.scalar.copy(ctxT[:, b, :], b_of(("ctxT", b))[0:DC, :]).then_inc(free(("ctxT", b)), 1)

            def kv(b):
                if b == 0:
                    act.wait_ge(ld_kv, 48)
                is_full(act, ("k", b))
                nc.scalar.activation(kT[:, b, :], b_of(("k", b))[:], ACT.Identity,
                                     bias=bk_s[:, 0:1]).then_inc(free(("k", b)), 1)
                is_full(act, ("v", b))
                nc.scalar.copy(vx[:, b * KC:(b + 1) * KC, :].rearrange("p c d -> p (c d)"),
                               b_of(("v", b))[:]).then_inc(free(("v", b)), 1)

            ctx_turn(0)
            ctx_turn(1)
            kv(0)
            ctx_turn(2)
            kv(1)
            ctx_turn(3)
            kv(2)
            kv(3)

            for slot in range(SLOTS_X):
                i = slot
                if i < NT:
                    act.wait_ge(nb_ready, i + 1)
                    if i >= 2:
                        is_full(act, ("pT", i - 2))
                    nc.scalar.activation(probs[:, i % 2, :], b_of(("s", i))[:], ACT.Exp, bias=small[:, 1, i:i + 1],
                                         scale=SCALE_X, accum_out=small[:, 2, i:i + 1]).then_inc(free(("s", i)), 1)
                i = slot - 2
                if 0 <= i < NT:
                    is_full(act, ("pT", i))
                    if i >= 2:
                        is_full(act, ("o", i - 2))
                    nc.scalar.copy(probsT[:, i % 2].rearrange("p c t -> p (c t)"),
                                   b_of(("pT", i))[:]).then_inc(free(("pT", i)), 1)
                if slot >= 6 and slot % 2 == 0 and (slot - 6) // 2 < NB:
                    b = (slot - 6) // 2
                    is_full(act, ("hT", b))
                    if b == 0:
                        act.wait_ge(ld_ffn, 16 * 7)
                    nc.scalar.activation(xnT[:, b, :], b_of(("hT", b))[:, 0:L], ACT.Copy,
                                         scale=n1_s[:, 0:1]).then_inc(free(("hT", b)), 1)
                if slot >= 7 and slot % 2 == 1 and (slot - 7) // 2 < NB:
                    b = (slot - 7) // 2
                    is_full(act, ("qk2", b))
                    if b >= 2:
                        act.wait_ge(scratch_written[b - 2], 64)
                    nc.scalar.copy(split[:, b % 2, 0].rearrange("p q s -> p (q s)"),
                                   b_of(("qk2", b))[:]).then_inc(hi_ready, 1)
                    is_full(act, ("v2", b))
                    if b == 0:
                        act.wait_ge(vh_ready, 1)
                    nc.scalar.copy(vh[:, b * TB:(b + 1) * TB, :, 0:DH],
                                   b_of(("v2", b))[:, 0:TB * D].rearrange("p (t h d) -> p t h d", t=TB, h=NH)
                                   ).then_inc(free(("v2", b)), 1)

            def misc(step, b):
                if step == "mT":
                    is_full(act, ("mT", b))
                    if b >= 2:
                        act.wait_ge(m_placed[b - 2], 16)
                    nc.scalar.mul(negmT[:, b % 2, :], b_of(("mT", b))[0:NH, 0:L], -1.0).then_inc(free(("mT", b)), 1)
                if step == "cT":
                    is_full(act, ("cT", b))
                    nc.scalar.copy(cT[:], b_of(("cT", b))[:, 0:L]).then_inc(free(("cT", b)), 1)
                if step == "wo":
                    is_read(act, ("wo", b))
                    if b >= 1:
                        is_full(act, ("h2T", b - 1))
                    for j in range(TB):
                        i = b * TB + j
                        last = nc.scalar.activation(h2[:, j, :], y[:, i, :], ACT.Square, scale=float(D) ** -0.5,
                                                    accum_out=ms2[:, i:i + 1])
                        last.then_inc(ms2_ready, 1)
                if step == "h2T":
                    is_full(act, ("h2T", b))
                    nc.scalar.activation(h2T[:, b, :], b_of(("h2T", b))[:, 0:L], ACT.Copy,
                                         scale=n2_s[:, 0:1]).then_inc(free(("h2T", b)), 1)
                ts = slice(4 * (b // 2), 4 * (b // 2) + 4)
                if step == "route_exp1":
                    act.wait_ge(route_in, 2 * (b // 2) + 1)
                    nc.scalar.activation(rt[:, 3, ts, :], rt[:, 2, ts, :], ACT.Exp).then_inc(route_exp, 1)
                if step == "route_exp2":
                    act.wait_ge(route_in, 2 * (b // 2) + 2)
                    nc.scalar.activation(rs[:, 7, ts], rs[:, 6, ts], ACT.Exp).then_inc(route_exp, 1)

            for slot in range(SLOTS_A):
                n = slot - LAG
                if 0 <= n < NHEADS:
                    is_full(act, ("exp", n))
                    if n >= 3:
                        pv_done(act, n - 3)
                    nc.scalar.activation(ep[:, n % 3].rearrange("p t s -> p (t s)"), b_of(("exp", n))[:],
                                         ACT.Exp, scale=SCALE_H).then_inc(free(("exp", n)), 1)
                n = slot - PV_LAG - 1
                if 0 <= n < NHEADS and n % 4 == 3:
                    g = n // 4
                    is_full(act, ("pv", g))
                    if g >= NQ:
                        is_full(act, ("uT", g // NQ - 1, 1))
                    nc.scalar.copy(u[:, g % NQ, :], b_of(("pv", g))[:, 0:L]).then_inc(free(("pv", g)), 1)
                for step, b in misc_at.get(slot, []):
                    misc(step, b)

            for n in range(NI):
                for f in range(2):
                    is_full(act, ("gate", n, f))
                    if n >= 2:
                        is_read(act, ("up", n - 2, f))
                    nc.scalar.activation(silu[:, n % 2, f, :], b_of(("gate", n, f))[:],
                                         ACT.Silu).then_inc(free(("gate", n, f)), 1)

        @block.vector
        def _(dve):
            done = [0]

            def step(ins):
                done[0] += 1
                ins.then_inc(dve_step, 1)
                dve.wait_ge(dve_step, done[0])

            def norm_stats(k, b, src):
                for i in range(b * TB, (b + 1) * TB):
                    last = nc.vector.bn_stats(bn6[:, k, i, :], src[:, i, :])
                    last.then_inc(dve_step, 1)
                done[0] += TB
                dve.wait_ge(dve_step, done[0])
                for i in range(b * TB, (b + 1) * TB):
                    last = nc.vector.bn_aggr(mv[:, k, i, :], bn6[:, k, i, :])
                    last.then_inc(dve_step, 1)
                done[0] += TB
                dve.wait_ge(dve_step, done[0])

            def first_stats(b):
                dve.wait_ge(ld_x[b], 16)
                norm_stats(0, b, xs)
                ts = slice(b * TB, (b + 1) * TB)
                nc.vector.tensor_scalar(small[:, 0, ts], mv[:, 0, ts, 1], LN_EPS, None, ALU.add).then_inc(norm1_in, 1)

            def first_norm(b):
                dve.wait_ge(norm1_out, b + 1)
                for i in range(b * TB, (b + 1) * TB):
                    last = nc.vector.tensor_scalar(y[:, i, :], xs[:, i, :], mv[:, 0, i, 0:1], small[:, 8, i:i + 1],
                                                   ALU.subtract, ALU.mult)
                last.then_inc(xn_ready, 1)

            def xn_turn(b):
                is_full(dve, ("xnT", b))
                nc.vector.tensor_copy(xnT[:, b, :], b_of(("xnT", b))[:, 0:L]).then_inc(free(("xnT", b)), 1)

            def q_bias(b):
                if b == 0:
                    dve.wait_ge(ld_q, 32)
                is_full(dve, ("q", b))
                nc.vector.tensor_scalar(qT[:, b, :], b_of(("q", b))[:, 0:L], bq_s[:, 0:1], None,
                                        ALU.add).then_inc(free(("q", b)), 1)

            first_stats(0)
            first_stats(1)
            first_norm(0)
            first_stats(2)
            first_norm(1)
            xn_turn(0)
            first_stats(3)
            first_norm(2)
            q_bias(0)
            xn_turn(1)
            first_norm(3)
            q_bias(1)
            xn_turn(2)
            q_bias(2)
            xn_turn(3)
            q_bias(3)

            def second_stats(b):
                ts = slice(b * TB, (b + 1) * TB)
                norm_stats(1, b, x1)
                step(nc.vector.tensor_scalar(small[:, 3, ts], mv[:, 1, ts, 1], LN_EPS, None, ALU.add))
                step(nc.vector.reciprocal(small[:, 0, ts], small[:, 3, ts]))
                step(nc.vector.tensor_tensor(small[:, 4, ts], mv[:, 1, ts, 1], small[:, 0, ts], ALU.mult))
                nc.vector.tensor_scalar(small[:, 4, ts], small[:, 4, ts], RMS_EPS, None, ALU.add).then_inc(norm2_in, 1)

            def second_norm(b):
                dve.wait_ge(norm2_out, b + 1)
                for i in range(b * TB, (b + 1) * TB):
                    last = nc.vector.tensor_scalar(y[:, i, :], x1[:, i, :], mv[:, 1, i, 0:1], small[:, 5, i:i + 1],
                                                   ALU.subtract, ALU.mult)
                    last.then_inc(dve_step, 1)
                done[0] += TB
                dve.wait_ge(dve_step, done[0])
                for i in range(b * TB, (b + 1) * TB):
                    last = nc.vector.tensor_scalar(xs[:, i, :], y[:, i, :], small[:, 6, i:i + 1], None, ALU.mult)
                last.then_inc(hs_ready, 1)

            for slot in range(SLOTS_X):
                i = slot
                if i < NT:
                    is_full(dve, ("s", i))
                    step(nc.vector.reduce_max(small[:, 7, i:i + 1], b_of(("s", i))[:], AX_X))
                    nc.vector.tensor_scalar(small[:, 1, i:i + 1], small[:, 7, i:i + 1], -SCALE_X, None,
                                            ALU.mult).then_inc(nb_ready, 1)
                i = slot - 3
                if 0 <= i < NT:
                    is_read(dve, ("s", i))
                    if i == 0:
                        dve.wait_ge(tg_ready, 1)
                    step(nc.vector.reciprocal(small[:, 9, i:i + 1], small[:, 2, i:i + 1]))
                    step(nc.vector.tensor_scalar(small[:, 10, i:i + 1], small[:, 9, i:i + 1], tg[:, 0:1], None, ALU.mult))
                    dve.wait_ge(xb_ready, i // TB + 1)
                    is_full(dve, ("o", i))
                    nc.vector.scalar_tensor_tensor(out=x1[:, i, :], in0=b_of(("o", i))[:, 0:D],
                                                   scalar=small[:, 10, i:i + 1], in1=xs[:, i, :],
                                                   op0=ALU.mult, op1=ALU.add).then_inc(free(("o", i)), 1)
                    if i % TB == TB - 1:
                        for t in range(TB):
                            bank, before = place[("o", i - t)]
                            dve.wait_ge(emptied[bank], before + 1)
                        second_stats(i // TB)
                        second_norm(i // TB)
                if slot >= 7 and slot % 2 == 1 and (slot - 7) // 2 < NB:
                    b = (slot - 7) // 2
                    dve.wait_ge(hi_ready, b + 1)
                    nc.vector.tensor_tensor(split[:, b % 2, 1].rearrange("p q s -> p (q s)"), b_of(("qk2", b))[:],
                                            split[:, b % 2, 0].rearrange("p q s -> p (q s)").bitcast(F32),
                                            ALU.subtract).then_inc(free(("qk2", b)), 1)

            def routing(kind, h):
                ts = slice(4 * h, 4 * h + 4)
                wide = [P, 4, NE]

                def spread(col):
                    return rs[:, col, ts].unsqueeze(2).broadcast_to(wide)

                lg, d1, ex, pr, eq, key, oh1, p2, oh2 = (rt[:, c, ts, :] for c in (1, 2, 3, 4, 5, 6, 7, 8, 9))
                order = widx[:].unsqueeze(1).broadcast_to(wide)
                if kind == "router":
                    is_read(dve, ("router", 2 * h + 1))
                    step(nc.vector.tensor_reduce(rs[:, 0, ts], lg, AX_X, ALU.max))
                    nc.vector.tensor_tensor(d1, lg, spread(0), ALU.subtract).then_inc(route_in, 1)
                if kind == "route_top":
                    dve.wait_ge(route_exp, 2 * h + 1)
                    step(nc.vector.tensor_reduce(rs[:, 1, ts], ex, AX_X, ALU.add))
                    step(nc.vector.reciprocal(rs[:, 2, ts], rs[:, 1, ts]))
                    step(nc.vector.tensor_tensor(pr, ex, spread(2), ALU.mult))
                    step(nc.vector.tensor_reduce(rs[:, 3, ts], pr, AX_X, ALU.max))
                    step(nc.vector.tensor_tensor(eq, pr, spread(3), ALU.is_equal))
                    step(nc.vector.tensor_tensor(key, eq, order, ALU.mult))
                    step(nc.vector.tensor_reduce(rs[:, 4, ts], key, AX_X, ALU.max))
                    step(nc.vector.tensor_tensor(oh1, order, spread(4), ALU.is_equal))
                    step(nc.vector.scalar_tensor_tensor(out=p2, in0=oh1, scalar=-2.0, in1=pr, op0=ALU.mult, op1=ALU.add))
                    step(nc.vector.tensor_reduce(rs[:, 5, ts], p2, AX_X, ALU.max))
                    nc.vector.tensor_tensor(rs[:, 6, ts], rs[:, 5, ts], rs[:, 3, ts], ALU.subtract).then_inc(route_in, 1)
                    step(nc.vector.tensor_tensor(eq, p2, spread(5), ALU.is_equal))
                    step(nc.vector.tensor_tensor(key, eq, order, ALU.mult))
                    step(nc.vector.tensor_reduce(rs[:, 8, ts], key, AX_X, ALU.max))
                    step(nc.vector.tensor_tensor(oh2, order, spread(8), ALU.is_equal))
                if kind == "route_weights":
                    dve.wait_ge(route_exp, 2 * h + 2)
                    step(nc.vector.tensor_scalar(rs[:, 9, ts], rs[:, 7, ts], 1.0, None, ALU.add))
                    step(nc.vector.reciprocal(rs[:, 10, ts], rs[:, 9, ts]))
                    step(nc.vector.tensor_scalar(rs[:, 10, ts], rs[:, 10, ts], tg[:, 1:2], None, ALU.mult))
                    step(nc.vector.tensor_tensor(rs[:, 11, ts], rs[:, 10, ts], rs[:, 7, ts], ALU.mult))
                    step(nc.vector.tensor_tensor(oh1, oh1, spread(10), ALU.mult))
                    step(nc.vector.tensor_tensor(oh2, oh2, spread(11), ALU.mult))
                    step(nc.vector.tensor_tensor(cw[:, ts, :], oh1, oh2, ALU.add))

            def misc(kind, b):
                ts = slice(b * TB, (b + 1) * TB)
                if kind == "uT":
                    for j in range(TB):
                        is_full(dve, ("uT", b, j))
                        heads = b_of(("uT", b, j))[:].rearrange("p (h c) -> p h c", c=32)
                        step(nc.vector.reciprocal(rden[:, j, :], heads[:, :, DH]))
                        if b >= 1 and j == 0:
                            is_full(dve, ("cT", b - 1))
                        last = nc.vector.tensor_tensor(cn[:, j], heads[:, :, 0:DH],
                                                       rden[:, j, :].unsqueeze(2).broadcast_to([P, NH, DH]), ALU.mult)
                        last.then_inc(free(("uT", b, j)), 1)
                if kind == "wo":
                    is_full(dve, ("wo", b))
                    yb = y[:, ts, :].rearrange("p t d -> p (t d)")
                    nc.vector.tensor_tensor(yb, b_of(("wo", b))[:, 0:TB * D], yb, ALU.add).then_inc(free(("wo", b)), 1)
                    is_read(dve, ("wo", b))
                    xb = x1[:, ts, :].rearrange("p t d -> p (t d)")
                    step(nc.vector.scalar_tensor_tensor(out=xb, in0=yb, scalar=tg[:, 1:2], in1=xb,
                                                        op0=ALU.mult, op1=ALU.add))
                    dve.wait_ge(norm3_out, b + 1)
                    for j in range(TB):
                        i = b * TB + j
                        last = nc.vector.tensor_scalar(h2[:, j, :], y[:, i, :], small[:, 11, i:i + 1], None, ALU.mult)
                    last.then_inc(h2_ready, 1)
                if kind == "router":
                    is_full(dve, ("router", b))
                    logits = b_of(("router", b))[:, 0:TB * P].rearrange("p (t e) -> p t e", t=TB)[:, :, 0:NE]
                    nc.vector.tensor_copy(rt[:, 1, ts, :], logits).then_inc(free(("router", b)), 1)
                    if b % 2:
                        routing(kind, b // 2)
                if kind in ("route_top", "route_weights"):
                    routing(kind, b // 2)

            for slot in range(SLOTS_A):
                n = slot
                if n < NHEADS:
                    is_full(dve, ("max", n))
                    nc.vector.tensor_reduce(mxs[:, n // NH, :, n % NH],
                                            b_of(("max", n))[:].rearrange("p (t s) -> p t s", t=TB),
                                            AX_X, ALU.max).then_inc(free(("max", n)), 1)
                for kind, b in misc_at.get(slot, []):
                    misc(kind, b)

            def accumulate(n):
                e, h = items[n]
                is_full(dve, ("down", n))
                for j in range(4):
                    i = 4 * h + j
                    c = tg[:, 1:2] if e == 0 else cw[:, i, e - 1:e]
                    last = nc.vector.scalar_tensor_tensor(out=x1[:, i, :], in0=b_of(("down", n))[:, j * D:(j + 1) * D],
                                                          scalar=c, in1=x1[:, i, :], op0=ALU.mult, op1=ALU.add)
                last.then_inc(free(("down", n)), 1)

            for n in range(NI):
                for f in range(2):
                    is_read(dve, ("gate", n, f))
                    is_full(dve, ("up", n, f))
                    if n >= 2:
                        is_full(dve, ("down", n - 2))
                    nc.vector.tensor_tensor(act_t[:, n % 2, f, :], silu[:, n % 2, f, :], b_of(("up", n, f))[:],
                                            ALU.mult).then_inc(free(("up", n, f)), 1)
                if n >= 1:
                    if n >= 2:
                        is_read(dve, ("down", n - 2))
                    accumulate(n - 1)
            is_read(dve, ("down", NI - 2))
            accumulate(NI - 1)

        @block.tensor
        def _(pe):
            def ctx_turn(b):
                pe.wait_ge(ld_ctx[b], 16)
                may_fill(pe, ("ctxT", b))
                for c in range(KC):
                    last = pe.transpose(b_of(("ctxT", b))[0:DC, c * P:(c + 1) * P], ctx_s[:, b * KC + c, :], ident[:])
                last.then_inc(full(("ctxT", b)), 1)

            def written(use):
                is_read(pe, use)

            def kv(b):
                written(("ctxT", b))
                may_fill(pe, ("k", b))
                pe.matmul(b_of(("k", b))[:], Wk_s[:], ctxT[:, b, :], start=True, stop=True).then_inc(full(("k", b)), 1)
                may_fill(pe, ("v", b))
                for c in range(KC):
                    last = pe.matmul(b_of(("v", b))[:, c * D:(c + 1) * D], ctxT[:, b, c * P:(c + 1) * P], Wv_s[:],
                                     start=True, stop=True)
                last.then_inc(full(("v", b)), 1)

            def xn_turn(b):
                pe.wait_ge(xn_ready, b + 1)
                may_fill(pe, ("xnT", b))
                for j in range(TB):
                    last = pe.transpose(b_of(("xnT", b))[:, j * P:(j + 1) * P], y[:, b * TB + j, :], ident[:])
                last.then_inc(full(("xnT", b)), 1)

            def q_proj(b):
                written(("xnT", b))
                may_fill(pe, ("q", b))
                pe.matmul(b_of(("q", b))[:, 0:L], Wq_s[:], xnT[:, b, :], start=True, stop=True
                          ).then_inc(full(("q", b)), 1)

            pe.wait_ge(ident_ready, 1)
            ctx_turn(0)
            ctx_turn(1)
            pe.wait_ge(ld_kv, 48)
            kv(0)
            xn_turn(0)
            ctx_turn(2)
            kv(1)
            pe.wait_ge(ld_q, 32)
            q_proj(0)
            xn_turn(1)
            ctx_turn(3)
            kv(2)
            q_proj(1)
            xn_turn(2)
            kv(3)
            q_proj(2)
            xn_turn(3)
            q_proj(3)

            for slot in range(SLOTS_X):
                i = slot
                if i < NT:
                    b = i // TB
                    if i % TB == 0:
                        written(("k", b))
                        written(("q", b))
                    may_fill(pe, ("s", i))
                    pe.matmul(b_of(("s", i))[:], qT[:, b, (i % TB) * P:(i % TB + 1) * P], kT[:, b, :],
                              start=True, stop=True).then_inc(full(("s", i)), 1)
                i = slot - 2
                if 0 <= i < NT:
                    is_read(pe, ("s", i))
                    may_fill(pe, ("pT", i))
                    for c in range(KC):
                        last = pe.transpose(b_of(("pT", i))[:, c * P:(c + 1) * P], probs[:, i % 2, c * P:(c + 1) * P],
                                            ident[:])
                    last.then_inc(full(("pT", i)), 1)
                i = slot - 3
                if 0 <= i < NT:
                    written(("pT", i))
                    written(("v", i // TB))
                    may_fill(pe, ("o", i))
                    for c in range(KC):
                        last = pe.matmul(b_of(("o", i))[:, 0:D], probsT[:, i % 2, c, :], vx[:, (i // TB) * KC + c, :],
                                         start=(c == 0), stop=(c == KC - 1))
                    last.then_inc(full(("o", i)), 1)
                if slot >= 6 and slot % 2 == 0 and (slot - 6) // 2 < NB:
                    b = (slot - 6) // 2
                    pe.wait_ge(hs_ready, b + 1)
                    may_fill(pe, ("hT", b))
                    for j in range(TB):
                        last = pe.transpose(b_of(("hT", b))[:, j * P:(j + 1) * P], xs[:, b * TB + j, :], ident[:])
                    last.then_inc(full(("hT", b)), 1)
                if slot >= 7 and slot % 2 == 1 and (slot - 7) // 2 < NB:
                    b = (slot - 7) // 2
                    written(("hT", b))
                    if b == 0:
                        pe.wait_ge(wqk_ready, 2)
                        pe.wait_ge(ld_ffn, 16 * 7)
                    may_fill(pe, ("qk2", b))
                    for i in range(2):
                        last = pe.matmul(b_of(("qk2", b))[:, i * L:(i + 1) * L], wqk[:, i, :], xnT[:, b, :],
                                         start=True, stop=True)
                    last.then_inc(full(("qk2", b)), 1)
                    may_fill(pe, ("v2", b))
                    for j in range(TB):
                        last = pe.matmul(b_of(("v2", b))[:, j * D:(j + 1) * D], xnT[:, b, j * P:(j + 1) * P], wv_s[:],
                                         start=True, stop=True)
                    last.then_inc(full(("v2", b)), 1)

            def misc(step, b):
                if step == "mT":
                    is_read(pe, ("max", NH * (b + 1) - 1))
                    may_fill(pe, ("mT", b))
                    for j in range(TB):
                        last = pe.transpose(b_of(("mT", b))[0:NH, j * P:(j + 1) * P], mxs[:, b, j, :], ident[:])
                    last.then_inc(full(("mT", b)), 1)
                if step == "uT":
                    is_read(pe, ("pv", NQ * (b + 1) - 1))
                    for j in range(TB):
                        may_fill(pe, ("uT", b, j))
                        for g in range(NQ):
                            last = pe.transpose(b_of(("uT", b, j))[:, g * P:(g + 1) * P], u[:, g, j * P:(j + 1) * P],
                                                ident[:])
                        last.then_inc(full(("uT", b, j)), 1)
                if step == "cT":
                    for j in range(TB):
                        written(("uT", b, j))
                    may_fill(pe, ("cT", b))
                    for j in range(TB):
                        last = pe.transpose(b_of(("cT", b))[:, j * P:(j + 1) * P], cn[:, j].rearrange("p h d -> p (h d)"),
                                            ident[:])
                    last.then_inc(full(("cT", b)), 1)
                if step == "wo":
                    written(("cT", b))
                    may_fill(pe, ("wo", b))
                    for j in range(TB):
                        last = pe.matmul(b_of(("wo", b))[:, j * D:(j + 1) * D], cT[:, j * P:(j + 1) * P], wo_s[:],
                                         start=True, stop=True)
                    last.then_inc(full(("wo", b)), 1)
                if step == "h2T":
                    pe.wait_ge(h2_ready, b + 1)
                    may_fill(pe, ("h2T", b))
                    for j in range(TB):
                        last = pe.transpose(b_of(("h2T", b))[:, j * P:(j + 1) * P], h2[:, j, :], ident[:])
                    last.then_inc(full(("h2T", b)), 1)
                if step == "router":
                    is_read(pe, ("h2T", b))
                    if b == 0:
                        pe.wait_ge(router_ready, 1)
                    may_fill(pe, ("router", b))
                    for j in range(TB):
                        last = pe.matmul(b_of(("router", b))[:, j * P:(j + 1) * P], h2T[:, b, j * P:(j + 1) * P],
                                         router_pad[:], start=True, stop=True)
                    last.then_inc(full(("router", b)), 1)

            K = 96
            for slot in range(SLOTS_A):
                n = slot
                if n < NHEADS:
                    b, h = n // NH, n % NH
                    if h == 0:
                        pe.wait_ge(stacked[b], 128)
                    may_fill(pe, ("max", n))
                    for j in range(TB):
                        last = pe.matmul(b_of(("max", n))[:, j * L:(j + 1) * L],
                                         q_st[0:K, b % NSTACK, h // 2, j * P:(j + 1) * P],
                                         k_st[0:K, b % NSTACK, h, :], start=True, stop=True)
                    last.then_inc(full(("max", n)), 1)
                n = slot - LAG
                if 0 <= n < NHEADS:
                    b, h = n // NH, n % NH
                    if h == 0:
                        pe.wait_ge(m_placed[b], 16)
                    may_fill(pe, ("exp", n))
                    for j in range(TB):
                        last = pe.matmul(b_of(("exp", n))[:, j * L:(j + 1) * L],
                                         k_st[0:K, b % NSTACK, h, j * P:(j + 1) * P],
                                         q_st[0:K, b % NSTACK, h // 2, :], start=True, stop=True)
                    last.then_inc(full(("exp", n)), 1)
                n = slot - PV_LAG
                if 0 <= n < NHEADS:
                    b, h = n // NH, n % NH
                    is_read(pe, ("exp", n))
                    if h == 0:
                        written(("v2", b))
                    if n % 4 == 0:
                        may_fill(pe, ("pv", n // 4))
                    r = 32 * (n % 4)
                    for j in range(TB):
                        last = pe.matmul(b_of(("pv", n // 4))[r:r + 32, 0:L], vh[:, b * TB + j, h, :], ep[:, n % 3, j, :],
                                         start=(j == 0), stop=(j == TB - 1), tile_position=(0, r))
                    last.then_inc(pv_heads if n % 4 < 3 else full(("pv", n // 4)), 1)
                for step, b in misc_at.get(slot, []):
                    misc(step, b)

            def down_proj(n):
                e, h = items[n]
                is_read(pe, ("up", n, 1))
                may_fill(pe, ("down", n))
                for j in range(4):
                    for f in range(2):
                        last = pe.matmul(b_of(("down", n))[:, j * D:(j + 1) * D], act_t[:, n % 2, f, j * P:(j + 1) * P],
                                         down[:, e, f, :], start=(f == 0), stop=(f == 1))
                last.then_inc(full(("down", n)), 1)

            pe.wait_ge(ld_down, 16 * NEXP)
            for n, (e, h) in enumerate(items):
                pe.wait_ge(w_split, e + 1)
                pe.wait_ge(h2s_ready, 2 * h + 2)
                hs = slice(h * HALF, (h + 1) * HALF)
                for f in range(2):
                    fs = slice(f * P, (f + 1) * P)
                    for k, use in ((0, "gate"), (1, "up")):
                        may_fill(pe, (use, n, f))
                        bank = b_of((use, n, f))
                        pe.matmul(bank[:], whi[:, e % NSPLIT, k, fs], h2hi[:, hs], start=True, stop=False)
                        pe.matmul(bank[:], whi[:, e % NSPLIT, k, fs], h2lo[:, hs], start=False, stop=False)
                        last = pe.matmul(bank[:], wlo[:, e % NSPLIT, k, fs], h2hi[:, hs], start=False, stop=True)
                        last.then_inc(full((use, n, f)), 1)
                if n >= 1:
                    down_proj(n - 1)
            down_proj(NI - 1)


_INS = ["x", "ctx_768", "g_xattn", "g_ffn", "L0_xattn_Wq", "L0_xattn_bq", "L0_xattn_Wk", "L0_xattn_bk", "L0_xattn_Wv",
        "L0_xattn_bv", "L0_ffn_norm1_w", "L0_ffn_norm2_w", "L0_ffn_wq", "L0_ffn_wk", "L0_ffn_wv", "L0_ffn_wo",
        "L0_ffn_router_w", "L0_ffn_sh_gate", "L0_ffn_sh_up", "L0_ffn_sh_down", "L0_ffn_e_gate", "L0_ffn_e_up",
        "L0_ffn_e_down"]


def kernel(**inputs):
    import numpy as _np
    import concourse.bacc as _bacc
    from concourse import mybir as _mybir
    from concourse.bass_utils import run_bass_kernel_spmd as _run

    nc = _bacc.Bacc("TRN2", target_bir_lowering=False, num_devices=1)
    arrays, args = {}, []
    for name in _INS:
        a = _np.ascontiguousarray(inputs[name])
        arrays[f"in_{name}_dram"] = a
        args.append(nc.dram_tensor(f"in_{name}_dram", a.shape, _mybir.dt.from_np(a.dtype), kind="ExternalInput").ap())
    shape = tuple(inputs["x"].shape)
    args.append(nc.dram_tensor("out_0_dram", shape, _mybir.dt.from_np(_np.dtype("float32")), kind="ExternalOutput").ap())
    flamingo_block(nc, *args)
    r = _run(nc, [arrays], core_ids=[0])
    return r.results[0]["out_0_dram"]
```

```python
from contextlib import ExitStack

import concourse.bass as bass
from concourse import mybir

ALU = mybir.AluOpType
ACT = mybir.ActivationFunctionType
AX_X = mybir.AxisListType.X
F32 = mybir.dt.float32
F32R = mybir.dt.float32r

P = 128
LN_EPS = 1e-5
RMS_EPS = 1e-6
NSTACK = 3
LAG = 13
PV_LAG = LAG + 2
C_LAG = PV_LAG + 16
A_FROM = 9
A_PER_X = 4
M_FROM = 64
NEARLY = 3
WARM = 12
NSPLIT = 3
NRAW = 3


def bank_uses(pairs):
    place = {}
    for banks, uses in pairs:
        for n, use in enumerate(uses):
            place[use] = (banks[n % len(banks)], n // len(banks))
    return place


def flamingo_block(nc, x_tiles, ctx_T, attn_w, ffn_w, expert_w, out, NB, L):
    D = x_tiles.shape[2]
    DC, _, LK = ctx_T.shape
    NEXP, _, EW = expert_w.shape
    NE = NEXP - 1
    FF = EW // 3
    NT = NB * L // P
    TB = L // P
    KC = LK // P
    DH = 8
    NH = D // DH
    NG = NH // 2
    NQ = NH // 4
    SCALE_X = float(D) ** -0.5
    SCALE_H = float(DH) ** -0.5
    NHEADS = NB * NH
    HALF = NB * L // 2

    scratch = nc.dram_tensor("split_scratch", [NB, 2, 2, 2, DH, NG, L], F32, kind="Internal").ap()

    SLOTS_X = NT + 5
    misc_at = {}
    for b in range(NB):
        misc_at.setdefault(16 * b + 9, []).append(("mT0", b))
        misc_at.setdefault(16 * b + 17, []).append(("mT1", b))
        steps = [(0, "uT"), (2, "cT"), (4, "wo"), (5, "square"), (7, "h2"), (8, "h2T"), (10, "router")]
        if b % 2:
            steps += [(11, "route_exp1"), (12, "route_top"), (14, "route_exp2"), (15, "route_weights")]
        for off, step in steps:
            misc_at.setdefault(16 * b + C_LAG + off, []).append((step, b))
    SLOTS_A = max(misc_at) + 1
    items = [(e, h) for h in range(2) for e in range(NEARLY)] + [(e, h) for e in range(NEARLY, NEXP) for h in range(2)]
    NI = len(items)
    last_item_of = {e: max(n for n, it in enumerate(items) if it[0] == e) for e in range(NEXP)}
    thirds = [(n, k) for n in range(NI) for k in range(3)] + [(NI, 2)]

    order = [("x", i) for i in range(A_FROM)]
    a = 0
    for i in range(A_FROM, SLOTS_X):
        order += [("x", i)] + [("a", a + j) for j in range(A_PER_X)]
        a += A_PER_X
    early = 0
    for i in range(a, SLOTS_A):
        order.append(("a", i))
        if i >= M_FROM and (i - M_FROM) % 2 == 0 and early < 3 * NEARLY:
            order.append(("m", early))
            early += 1
    order += [("m", i) for i in range(early, len(thirds))]

    pair_uses = {"turn": [("xnT", 0)], "proj": [("k", 0), ("v", 0), ("q", 0)], "sum": [], "misc": []}
    for stage, i in order:
        if stage == "x":
            if i < NT:
                pair_uses["sum"].append(("s", i))
            if 0 <= i - 2 < NT:
                pair_uses["misc"].append(("o", i - 2))
            b = i // 2 + 1
            if i < NT and b < NB:
                if i % 2 == 0:
                    pair_uses["proj"] += [("k", b), ("v", b)]
                else:
                    pair_uses["turn"].append(("xnT", b))
                    pair_uses["proj"].append(("q", b))
            if 0 <= i - 1 < NT:
                pair_uses["turn"].append(("pT", i - 1))
            if i >= 5 and i % 2 == 1 and (i - 5) // 2 < NB:
                pair_uses["turn"].append(("hT", (i - 5) // 2))
            if i >= 6 and i % 2 == 0 and (i - 6) // 2 < NB:
                pair_uses["proj"] += [("qk2", (i - 6) // 2), ("v2", (i - 6) // 2)]
        if stage == "a":
            if i < NHEADS:
                pair_uses["turn"].append(("max", i))
            if 0 <= i - LAG < NHEADS:
                pair_uses["proj"].append(("exp", i - LAG))
            if 0 <= i - PV_LAG < NHEADS and (i - PV_LAG) % 4 == 0:
                pair_uses["sum"].append(("pv", (i - PV_LAG) // 4))
            for step, b in misc_at.get(i, []):
                if step == "uT":
                    pair_uses["misc"] += [("uT", b, 0), ("uT", b, 1)]
                elif step in ("mT0", "mT1"):
                    pair_uses["misc"].append(("mT", b, int(step[2])))
                elif step in ("cT", "wo", "h2T", "router"):
                    pair_uses["misc"].append((step, b))
        if stage == "m":
            n, k = thirds[i]
            if k < 2:
                pair_uses["turn"].append(("gate", n, k))
                pair_uses["proj"].append(("up", n, k))
            elif n >= 1:
                pair_uses["sum"].append(("down", n - 1))
    place = bank_uses([((0, 1), pair_uses["turn"]), ((2, 3), pair_uses["proj"]),
                       ((4, 5), pair_uses["sum"]), ((6, 7), pair_uses["misc"])])

    with ExitStack() as ctx:
        def sb(name, shape, dt=F32):
            return ctx.enter_context(nc.sbuf_tensor(name, shape, dt))

        def sem(name):
            return ctx.enter_context(nc.semaphore(name))

        banks = [ctx.enter_context(nc.psum_tensor(f"bank{i}", [P, 512], F32)) for i in range(8)]
        filled = [sem(f"filled{i}") for i in range(8)]
        emptied = [sem(f"emptied{i}") for i in range(8)]

        ident = sb("ident", [P, P])
        tg = sb("tg", [P, 2])
        warm = sb("warm", [P, 512], F32R)
        attn_s = sb("attn_s", [P, 4 * D + 4])
        Wk_s, Wv_s, Wq_s, bv_row = (attn_s[:, i * D:(i + 1) * D] for i in range(4))
        bk_s, bq_s = attn_s[:, 4 * D:4 * D + 1], attn_s[:, 4 * D + 1:4 * D + 2]
        gates = attn_s[:, 4 * D + 2:4 * D + 4]
        ffn_s = sb("ffn_s", [P, 4 * D + NE + 2])
        wqk = ffn_s[:, 0:2 * D].rearrange("k (i m) -> k i m", i=2)
        wv_s, wo_s = ffn_s[:, 2 * D:3 * D], ffn_s[:, 3 * D:4 * D]
        router_s = ffn_s[:, 4 * D:4 * D + NE]
        n1_s, n2_s = ffn_s[:, 4 * D + NE:4 * D + NE + 1], ffn_s[:, 4 * D + NE + 1:4 * D + NE + 2]
        router_pad = sb("router_pad", [D, P])

        xs = sb("xs", [P, NT, D])
        x1 = sb("x1", [P, NT, D])
        y = sb("y", [P, NT, D])
        ctxT = sb("ctxT", [DC, NB, LK])
        kT = sb("kT", [D, NB, LK])
        vx = sb("vx", [P, NB * KC, D])
        qT = sb("qT", [D, NB, L])
        xnT = sb("xnT", [D, NB, L])
        probs = sb("probs", [P, 2, LK])
        probsT = sb("probsT", [P, 2, KC, P])
        bn6 = sb("bn6", [P, 2, NT, 6])
        mv = sb("mv", [P, 2, NT, 2])
        small = sb("small", [P, 12, NT])
        neg_half = sb("neg_half", [P, 2, TB])
        ms2 = sb("ms2", [P, NT])
        split = sb("split", [P, 2, 2, 2, L], F32R)
        vh = sb("vh", [P, NT, NH, 32])
        q_st = sb("q_st", [P, NSTACK, NG, L], F32R)
        k_st = sb("k_st", [P, NSTACK, NH, L], F32R)
        mxs = sb("mxs", [P, NB, TB, NH])
        negmT = sb("negmT", [NH // 2, 2, L], F32R)
        ep = sb("ep", [P, 3, TB, L])
        u = probsT[:].rearrange("p n c t -> p (n c t)").rearrange("p (g s) -> p g s", g=NQ)
        rden = sb("rden", [P, TB, NH])
        cn = sb("cn", [P, TB, NH, DH])
        cT = sb("cT", [D, L])
        h2 = sb("h2", [P, TB, D])
        h2T = probs[:].rearrange("p n s -> p (n s)").rearrange("p (b s) -> p b s", b=NB)
        h2hi, h2lo = sb("h2hi", [D, NB * L], F32R), sb("h2lo", [D, NB * L], F32R)
        rt = sb("rt", [P, 12, NT, NE])
        rs = sb("rs", [P, 12, NT])
        widx = sb("widx", [P, NE])
        cw = sb("cw", [P, NT, NE])
        raw = sb("raw", [P, NRAW, 3, FF])
        whi, wlo = sb("whi", [D, NSPLIT, 2, FF], F32R), sb("wlo", [D, NSPLIT, 2, FF], F32R)
        silu = kT[:].rearrange("p b t -> p (b t)").rearrange("p (n f t) -> p n f t", n=2, f=2)
        act_t = vx[:].rearrange("p a d -> p (a d)").rearrange("p (n f t) -> p n f t", n=2, f=2)

        ld_x = [sem(f"ld_x{i}") for i in range(2)]
        ld_ctx = [sem(f"ld_ctx{i}") for i in range(2)]
        ld_attn, ld_ffn = sem("ld_attn"), sem("ld_ffn")
        ld_raw = [sem(f"ld_raw{e}") for e in range(NRAW)]
        pads_copied = sem("pads_copied")
        scratch_written = [sem(f"scratch_written{b}") for b in range(NB)]
        stacked = [sem(f"stacked{b}") for b in range(NB)]
        m_placed = [sem(f"m_placed{i}") for i in range(2 * NB)]
        out_stored = sem("out_stored")
        pool_step, dve_step = sem("pool_step"), sem("dve_step")
        ident_ready, tg_ready, xb_ready = sem("ident_ready"), sem("tg_ready"), sem("xb_ready")
        router_ready, vh_ready, zeros_ready, pick_ready = sem("router_ready"), sem("vh_ready"), sem("zeros_ready"), sem("pick_ready")
        m_rows_zero = sem("m_rows_zero")
        xn_ready, hs_ready, hi_ready = sem("xn_ready"), sem("hs_ready"), sem("hi_ready")
        nb_ready = sem("nb_ready")
        norm1_in, norm1_out, norm2_in, norm2_out, norm3_out = (
            sem("norm1_in"), sem("norm1_out"), sem("norm2_in"), sem("norm2_out"), sem("norm3_out"))
        ms2_ready, h2_ready, h2s_ready, w_split = sem("ms2_ready"), sem("h2_ready"), sem("h2s_ready"), sem("w_split")
        tanh_ready, warm_ready = sem("tanh_ready"), sem("warm_ready")
        pv_heads, route_in, route_exp = sem("pv_heads"), sem("route_in"), sem("route_exp")

        def b_of(use):
            return banks[place[use][0]]

        def may_fill(eng, use):
            bank, before = place[use]
            if before:
                eng.wait_ge(emptied[bank], before)

        def full(use):
            return filled[place[use][0]]

        def is_full(eng, use):
            bank, before = place[use]
            eng.wait_ge(filled[bank], before + 1)

        def free(use):
            return emptied[place[use][0]]

        def is_read(eng, use):
            bank, before = place[use]
            eng.wait_ge(emptied[bank], before + 1)

        def pv_done(eng, n):
            if n % 4 == 3:
                is_full(eng, ("pv", n // 4))
            else:
                eng.wait_ge(pv_heads, 3 * (n // 4) + n % 4 + 1)

        block = ctx.enter_context(nc.Block())

        def load_raw(sp, e):
            sp.dma_start(raw[:, e % NRAW].rearrange("p k f -> p (k f)"), expert_w[e]).then_inc(ld_raw[e % NRAW], 16)

        def stack(sp, b):
            s = b % NSTACK
            is_read(sp, ("qk2", b))
            for qk in range(2):
                for part in range(2):
                    sp.dma_start(scratch[b, qk, :, part].rearrange("p d g s -> p (d g) s"),
                                 split[:, b % 2, part, qk, :].bitcast(F32)).then_inc(scratch_written[b], 16)
            sp.wait_ge(scratch_written[b], 64)
            if b == 0:
                sp.wait_ge(zeros_ready, 1)
                sp.wait_ge(pick_ready, 1)
            elif b >= NSTACK:
                sp.wait_ge(m_rows_zero, b - NSTACK + 1)
            for p in range(2):
                for a in range(2):
                    r = 32 * p + 16 * a
                    q_src = scratch[b, 0, p, a].rearrange("d g s -> d (g s)").unsqueeze(0).broadcast_to([2, DH, NG * L])
                    sp.dma_start(q_st[r:r + 16, s].rearrange("r g s -> r (g s)").bitcast(F32),
                                 q_src).then_inc(stacked[b], 16)
                    k_src = scratch[b, 1, p].rearrange("c d g s -> (c d) g s")
                    sp.dma_start(k_st[r:r + 16, s, p::2, :].bitcast(F32), k_src).then_inc(stacked[b], 16)

        def place_m(sp, b, half):
            is_read(sp, ("mT", b, half))
            is_read(sp, ("max", NH * b + 8 * half + 7))
            i, r = 2 * b + half, 64 + 8 * half
            src = negmT[:, i % 2, :].bitcast(F32).unsqueeze(1).broadcast_to([NH // 2, NG // 2, L])
            sp.dma_start(q_st[r:r + 8, b % NSTACK, 4 * half:4 * half + 4, :].bitcast(F32), src).then_inc(m_placed[i], 16)

        @block.sync
        def _(sp):
            sp.dma_start(ctxT[:, 0:1], ctx_T[:, 0:1]).then_inc(ld_ctx[0], 16)
            sp.dma_start(attn_s[:], attn_w).then_inc(ld_attn, 16)
            sp.dma_start(xs[:, 0:4], x_tiles[:, 0:4]).then_inc(ld_x[0], 16)
            sp.dma_start(xs[:, 4:8], x_tiles[:, 4:8]).then_inc(ld_x[1], 16)
            sp.dma_start(ctxT[:, 1:4], ctx_T[:, 1:4]).then_inc(ld_ctx[1], 16)
            sp.dma_start(ffn_s[:], ffn_w).then_inc(ld_ffn, 16)
            for e in range(NRAW):
                load_raw(sp, e)
            sp.wait_ge(zeros_ready, 1)
            sp.wait_ge(pick_ready, 1)
            k_words, q_words = k_st[:].bitcast(F32), q_st[:].bitcast(F32)
            for s in range(1, NSTACK):
                sp.dma_start(k_words[0:32, s, 1::2], k_words[0:32, 0, 1::2]).then_inc(pads_copied, 16)
                sp.dma_start(k_words[32:64, s, 0::2], k_words[32:64, 0, 0::2]).then_inc(pads_copied, 16)
                sp.dma_start(k_words[64:P, s], k_words[64:P, 0]).then_inc(pads_copied, 16)
                sp.dma_start(q_words[64:P, s], q_words[64:P, 0]).then_inc(pads_copied, 16)
            sp.wait_ge(pads_copied, 64 * (NSTACK - 1))
            stack(sp, 0)
            stack(sp, 1)
            place_m(sp, 0, 0)
            stack(sp, 2)
            place_m(sp, 0, 1)
            place_m(sp, 1, 0)
            stack(sp, 3)
            for i in range(3, 8):
                place_m(sp, i // 2, i % 2)
            for e in range(NRAW, NEXP):
                is_full(sp, ("down", last_item_of[e - NRAW]))
                load_raw(sp, e)
            for h in range(2):
                is_read(sp, ("down", NI - 2 + h))
                sp.dma_start(out[:, h * 4:h * 4 + 4], x1[:, h * 4:h * 4 + 4]).then_inc(out_stored, 16)
            sp.wait_ge(out_stored, 32)

        @block.gpsimd
        def _(pool):
            done = [0]

            def step(ins):
                done[0] += 1
                ins.then_inc(pool_step, 1)
                pool.wait_ge(pool_step, done[0])

            step(nc.gpsimd.memset(ident[:], 0.0))
            nc.gpsimd.affine_select(out=ident[:], in_=ident[:], compare_op=ALU.not_equal, fill=1.0, base=0,
                                    pattern=[[-1, P]], channel_multiplier=1).then_inc(ident_ready, 1)
            step(nc.gpsimd.memset(neg_half[:], -0.5))
            nc.gpsimd.memset(router_pad[:], 0.0).then_inc(pool_step, 1)
            for i in range(NE):
                last = nc.gpsimd.memset(widx[:, i:i + 1], float(NE - i))
            last.then_inc(pool_step, 1)
            done[0] += 2
            pool.wait_ge(ident_ready, 1)

            k_words = k_st[:, 0].bitcast(F32)
            pool.wait_ge(pool_step, done[0])
            step(nc.gpsimd.memset(k_words[0:32, 1::2], 0.0))
            step(nc.gpsimd.memset(k_words[32:64, 0::2], 0.0))
            nc.gpsimd.memset(q_st[64:P, 0].bitcast(F32), 0.0).then_inc(zeros_ready, 1)
            pool.wait_ge(zeros_ready, 1)

            def norm1(b):
                ts = slice(b * TB, (b + 1) * TB)
                pool.wait_ge(norm1_in, b + 1)
                nc.gpsimd.tensor_tensor(small[:, 8, ts], small[:, 0, ts], neg_half[:, 0], ALU.pow).then_inc(norm1_out, 1)

            def norm2(b):
                ts = slice(b * TB, (b + 1) * TB)
                pool.wait_ge(norm2_in, b + 1)
                nc.gpsimd.tensor_tensor(small[:, 5:7, ts], small[:, 3:5, ts], neg_half[:], ALU.pow).then_inc(norm2_out, 1)

            def norm3(b):
                ts = slice(b * TB, (b + 1) * TB)
                pool.wait_ge(ms2_ready, TB * (b + 1))
                step(nc.gpsimd.tensor_scalar(small[:, 7, ts], ms2[:, ts], RMS_EPS, None, ALU.add))
                nc.gpsimd.tensor_tensor(small[:, 11, ts], small[:, 7, ts], neg_half[:, 0], ALU.pow).then_inc(norm3_out, 1)

            for b in range(NB):
                norm1(b)
            pool.wait_ge(ld_attn, 16)
            pool.wait_ge(tg_ready, 1)
            step(nc.gpsimd.tensor_scalar(bv_row, bv_row, tg[:, 0:1], None, ALU.mult))
            for b in range(NB):
                pool.wait_ge(ld_x[b // 2], 16)
                pool.wait_ge(xn_ready, b + 1)
                xb = xs[:, b * TB:(b + 1) * TB, :]
                nc.gpsimd.tensor_tensor(xb, xb, bv_row.unsqueeze(1).broadcast_to([P, TB, D]),
                                        ALU.add).then_inc(xb_ready, 1)
            pool.wait_ge(ld_ffn, 16)
            pool.wait_ge(pool_step, done[0])
            nc.gpsimd.tensor_copy(router_pad[:, 0:NE], router_s).then_inc(router_ready, 1)
            step(nc.gpsimd.memset(vh[:, 0:4], 0.0))
            step(nc.gpsimd.memset(vh[:, 4:8], 0.0))
            nc.gpsimd.memset(vh[:, :, :, DH:DH + 1], 1.0).then_inc(vh_ready, 1)

            def split_weights(e):
                pool.wait_ge(ld_raw[e % NRAW], 16 * (e // NRAW + 1))
                if e >= NSPLIT:
                    is_full(pool, ("up", last_item_of[e - NSPLIT], 1))
                step(nc.gpsimd.tensor_copy(whi[:, e % NSPLIT], raw[:, e % NRAW, 0:2]))
                nc.gpsimd.tensor_tensor(wlo[:, e % NSPLIT], raw[:, e % NRAW, 0:2], whi[:, e % NSPLIT].bitcast(F32),
                                        ALU.subtract).then_inc(w_split, 1)

            norm2(0)
            split_weights(0)
            norm2(1)
            split_weights(1)
            norm2(2)
            norm2(3)
            split_weights(2)

            def split_h2(b):
                is_read(pool, ("h2T", b))
                step(nc.gpsimd.tensor_copy(h2hi[:, b * L:(b + 1) * L], h2T[:, b, :]))
                nc.gpsimd.tensor_tensor(h2lo[:, b * L:(b + 1) * L], h2T[:, b, :],
                                        h2hi[:, b * L:(b + 1) * L].bitcast(F32), ALU.subtract).then_inc(h2s_ready, 1)

            for b in range(NB - NSTACK):
                is_read(pool, ("exp", NH * (b + 1) - 1))
                pool.wait_ge(w_split, NSPLIT)
                nc.gpsimd.memset(q_st[64:96, b % NSTACK].bitcast(F32), 0.0).then_inc(m_rows_zero, 1)
                pool.wait_ge(m_rows_zero, b + 1)
            for b in range(NB):
                norm3(b)
                split_h2(b)
            for e in range(NSPLIT, NEXP):
                split_weights(e)

        @block.scalar
        def _(act):
            act.wait_ge(ld_attn, 16)
            nc.scalar.activation(tg[:], gates, ACT.Tanh).then_inc(tg_ready, 1)

            def kv(b):
                is_full(act, ("k", b))
                nc.scalar.activation(kT[:, b, :], b_of(("k", b))[:], ACT.Identity,
                                     bias=bk_s).then_inc(free(("k", b)), 1)
                is_full(act, ("v", b))
                nc.scalar.copy(vx[:, b * KC:(b + 1) * KC, :].rearrange("p c d -> p (c d)"),
                               b_of(("v", b))[:]).then_inc(free(("v", b)), 1)

            act.wait_ge(ident_ready, 1)
            pick = ident[64:P, 64:64 + NH].unsqueeze(2).broadcast_to([64, NH, L])
            kv(0)
            nc.scalar.copy(k_st[64:P, 0, :, :], pick).then_inc(pick_ready, 1)

            def x_slot(slot):
                i = slot
                if i < NT:
                    act.wait_ge(nb_ready, i + 1)
                    if i >= 2:
                        is_full(act, ("pT", i - 2))
                    nc.scalar.activation(probs[:, i % 2, :], b_of(("s", i))[:], ACT.Exp, bias=small[:, 1, i:i + 1],
                                         scale=SCALE_X, accum_out=small[:, 2, i:i + 1]).then_inc(free(("s", i)), 1)
                    if i % 2 == 0 and i // 2 + 1 < NB:
                        kv(i // 2 + 1)
                i = slot - 1
                if 0 <= i < NT:
                    is_full(act, ("pT", i))
                    if i >= 2:
                        is_full(act, ("o", i - 2))
                    nc.scalar.copy(probsT[:, i % 2].rearrange("p c t -> p (c t)"),
                                   b_of(("pT", i))[:]).then_inc(free(("pT", i)), 1)
                if slot >= 5 and slot % 2 == 1 and (slot - 5) // 2 < NB:
                    b = (slot - 5) // 2
                    is_full(act, ("hT", b))
                    if b == 0:
                        act.wait_ge(ld_ffn, 16)
                    nc.scalar.activation(xnT[:, b, :], b_of(("hT", b))[:, 0:L], ACT.Copy,
                                         scale=n1_s).then_inc(free(("hT", b)), 1)
                if slot >= 6 and slot % 2 == 0 and (slot - 6) // 2 < NB:
                    b = (slot - 6) // 2
                    is_full(act, ("qk2", b))
                    if b >= 2:
                        act.wait_ge(scratch_written[b - 2], 64)
                    nc.scalar.copy(split[:, b % 2, 0].rearrange("p q s -> p (q s)"),
                                   b_of(("qk2", b))[:]).then_inc(hi_ready, 1)
                    is_full(act, ("v2", b))
                    if b == 0:
                        act.wait_ge(vh_ready, 1)
                    nc.scalar.copy(vh[:, b * TB:(b + 1) * TB, :, 0:DH],
                                   b_of(("v2", b))[:, 0:TB * D].rearrange("p (t h d) -> p t h d", t=TB, h=NH)
                                   ).then_inc(free(("v2", b)), 1)

            def misc(step, b):
                if step in ("mT0", "mT1"):
                    half = int(step[2])
                    i, use = 2 * b + half, ("mT", b, half)
                    is_full(act, use)
                    if i >= 2:
                        act.wait_ge(m_placed[i - 2], 16)
                    nc.scalar.mul(negmT[:, i % 2, :], b_of(use)[0:NH // 2, 0:L], -1.0).then_inc(free(use), 1)
                if step == "cT":
                    is_full(act, ("cT", b))
                    nc.scalar.copy(cT[:], b_of(("cT", b))[:, 0:L]).then_inc(free(("cT", b)), 1)
                if step == "square":
                    is_read(act, ("wo", b))
                    if b >= 1:
                        is_full(act, ("h2T", b - 1))
                    for j in range(TB):
                        i = b * TB + j
                        last = nc.scalar.activation(h2[:, j, :], y[:, i, :], ACT.Square, scale=float(D) ** -0.5,
                                                    accum_out=ms2[:, i:i + 1])
                        last.then_inc(ms2_ready, 1)
                if step == "h2T":
                    is_full(act, ("h2T", b))
                    nc.scalar.activation(h2T[:, b, :], b_of(("h2T", b))[:, 0:L], ACT.Copy,
                                         scale=n2_s).then_inc(free(("h2T", b)), 1)
                ts = slice(4 * (b // 2), 4 * (b // 2) + 4)
                if step == "route_exp1":
                    act.wait_ge(route_in, 2 * (b // 2) + 1)
                    nc.scalar.activation(rt[:, 3, ts, :], rt[:, 2, ts, :], ACT.Exp).then_inc(route_exp, 1)
                if step == "route_exp2":
                    act.wait_ge(route_in, 2 * (b // 2) + 2)
                    nc.scalar.activation(rs[:, 7, ts], rs[:, 6, ts], ACT.Exp).then_inc(route_exp, 1)

            def a_slot(slot):
                n = slot - LAG
                if 0 <= n < NHEADS:
                    is_full(act, ("exp", n))
                    if n >= 3:
                        pv_done(act, n - 3)
                    nc.scalar.activation(ep[:, n % 3].rearrange("p t s -> p (t s)"), b_of(("exp", n))[:],
                                         ACT.Exp, scale=SCALE_H).then_inc(free(("exp", n)), 1)
                n = slot - PV_LAG - 1
                if 0 <= n < NHEADS and n % 4 == 3:
                    g = n // 4
                    is_full(act, ("pv", g))
                    if g >= NQ:
                        is_full(act, ("uT", g // NQ - 1, 1))
                    nc.scalar.copy(u[:, g % NQ, :], b_of(("pv", g))[:, 0:L]).then_inc(free(("pv", g)), 1)
                for step, b in misc_at.get(slot, []):
                    misc(step, b)

            def m_third(n, k):
                if k == 2:
                    return
                is_full(act, ("gate", n, k))
                if n >= 2:
                    is_read(act, ("up", n - 2, k))
                if n < NEARLY:
                    nc.scalar.activation(silu[:, n % 2, k, :], b_of(("gate", n, k))[:], ACT.Tanh,
                                         scale=0.5).then_inc(tanh_ready, 1)
                else:
                    nc.scalar.activation(silu[:, n % 2, k, :], b_of(("gate", n, k))[:],
                                         ACT.Silu).then_inc(free(("gate", n, k)), 1)

            for stage, i in order:
                if stage == "x":
                    x_slot(i)
                elif stage == "a":
                    a_slot(i)
                else:
                    m_third(*thirds[i])

        @block.vector
        def _(dve):
            done = [0]

            def step(ins):
                done[0] += 1
                ins.then_inc(dve_step, 1)
                dve.wait_ge(dve_step, done[0])

            def norm_stats(k, b, src):
                for i in range(b * TB, (b + 1) * TB):
                    last = nc.vector.bn_stats(bn6[:, k, i, :], src[:, i, :])
                    last.then_inc(dve_step, 1)
                done[0] += TB
                dve.wait_ge(dve_step, done[0])
                for i in range(b * TB, (b + 1) * TB):
                    last = nc.vector.bn_aggr(mv[:, k, i, :], bn6[:, k, i, :])
                    last.then_inc(dve_step, 1)
                done[0] += TB
                dve.wait_ge(dve_step, done[0])

            def first_stats(b):
                dve.wait_ge(ld_x[b // 2], 16)
                norm_stats(0, b, xs)
                ts = slice(b * TB, (b + 1) * TB)
                nc.vector.tensor_scalar(small[:, 0, ts], mv[:, 0, ts, 1], LN_EPS, None, ALU.add).then_inc(norm1_in, 1)

            def first_norm(b):
                dve.wait_ge(norm1_out, b + 1)
                for i in range(b * TB, (b + 1) * TB):
                    last = nc.vector.tensor_scalar(y[:, i, :], xs[:, i, :], mv[:, 0, i, 0:1], small[:, 8, i:i + 1],
                                                   ALU.subtract, ALU.mult)
                last.then_inc(xn_ready, 1)

            def xn_turn(b):
                is_full(dve, ("xnT", b))
                nc.vector.tensor_copy(xnT[:, b, :], b_of(("xnT", b))[:, 0:L]).then_inc(free(("xnT", b)), 1)

            def q_bias(b):
                if b == 0:
                    dve.wait_ge(ld_attn, 16)
                is_full(dve, ("q", b))
                nc.vector.tensor_scalar(qT[:, b, :], b_of(("q", b))[:, 0:L], bq_s, None,
                                        ALU.add).then_inc(free(("q", b)), 1)

            nc.vector.memset(warm[:].bitcast(F32), 0.0).then_inc(warm_ready, 1)
            first_stats(0)
            first_stats(1)
            first_norm(0)
            xn_turn(0)
            first_norm(1)
            q_bias(0)

            def second_stats(b):
                ts = slice(b * TB, (b + 1) * TB)
                norm_stats(1, b, x1)
                step(nc.vector.tensor_scalar(small[:, 3, ts], mv[:, 1, ts, 1], LN_EPS, None, ALU.add))
                step(nc.vector.reciprocal(small[:, 0, ts], small[:, 3, ts]))
                step(nc.vector.tensor_tensor(small[:, 4, ts], mv[:, 1, ts, 1], small[:, 0, ts], ALU.mult))
                nc.vector.tensor_scalar(small[:, 4, ts], small[:, 4, ts], RMS_EPS, None, ALU.add).then_inc(norm2_in, 1)

            def second_norm(b):
                dve.wait_ge(norm2_out, b + 1)
                for i in range(b * TB, (b + 1) * TB):
                    last = nc.vector.tensor_scalar(y[:, i, :], x1[:, i, :], mv[:, 1, i, 0:1], small[:, 5, i:i + 1],
                                                   ALU.subtract, ALU.mult)
                    last.then_inc(dve_step, 1)
                done[0] += TB
                dve.wait_ge(dve_step, done[0])
                for i in range(b * TB, (b + 1) * TB):
                    last = nc.vector.tensor_scalar(xs[:, i, :], y[:, i, :], small[:, 6, i:i + 1], None, ALU.mult)
                last.then_inc(hs_ready, 1)

            def x_slot(slot):
                i = slot
                if i < NT:
                    is_full(dve, ("s", i))
                    step(nc.vector.reduce_max(small[:, 7, i:i + 1], b_of(("s", i))[:], AX_X))
                    nc.vector.tensor_scalar(small[:, 1, i:i + 1], small[:, 7, i:i + 1], -SCALE_X, None,
                                            ALU.mult).then_inc(nb_ready, 1)
                    b = i // 2 + 1
                    if i % 2 == 0 and b + 1 < NB:
                        first_stats(b + 1)
                    if i % 2 == 1 and b < NB:
                        xn_turn(b)
                        if b + 1 < NB:
                            first_norm(b + 1)
                        q_bias(b)
                i = slot - 2
                if 0 <= i < NT:
                    is_read(dve, ("s", i))
                    if i == 0:
                        dve.wait_ge(tg_ready, 1)
                    step(nc.vector.reciprocal(small[:, 9, i:i + 1], small[:, 2, i:i + 1]))
                    step(nc.vector.tensor_scalar(small[:, 10, i:i + 1], small[:, 9, i:i + 1], tg[:, 0:1], None, ALU.mult))
                    dve.wait_ge(xb_ready, i // TB + 1)
                    is_full(dve, ("o", i))
                    nc.vector.scalar_tensor_tensor(out=x1[:, i, :], in0=b_of(("o", i))[:, 0:D],
                                                   scalar=small[:, 10, i:i + 1], in1=xs[:, i, :],
                                                   op0=ALU.mult, op1=ALU.add).then_inc(free(("o", i)), 1)
                    if i % TB == TB - 1:
                        for t in range(TB):
                            is_read(dve, ("o", i - t))
                        second_stats(i // TB)
                if slot >= 4 and slot % 2 == 0 and (slot - 4) // 2 < NB:
                    second_norm((slot - 4) // 2)
                if slot >= 6 and slot % 2 == 0 and (slot - 6) // 2 < NB:
                    b = (slot - 6) // 2
                    dve.wait_ge(hi_ready, b + 1)
                    nc.vector.tensor_tensor(split[:, b % 2, 1].rearrange("p q s -> p (q s)"), b_of(("qk2", b))[:],
                                            split[:, b % 2, 0].rearrange("p q s -> p (q s)").bitcast(F32),
                                            ALU.subtract).then_inc(free(("qk2", b)), 1)

            def routing(kind, h):
                ts = slice(4 * h, 4 * h + 4)
                wide = [P, 4, NE]

                def spread(col):
                    return rs[:, col, ts].unsqueeze(2).broadcast_to(wide)

                lg, d1, ex, pr, eq, key, oh1, p2, oh2 = (rt[:, c, ts, :] for c in (1, 2, 3, 4, 5, 6, 7, 8, 9))
                order = widx[:].unsqueeze(1).broadcast_to(wide)
                if kind == "router":
                    is_read(dve, ("router", 2 * h + 1))
                    step(nc.vector.tensor_reduce(rs[:, 0, ts], lg, AX_X, ALU.max))
                    nc.vector.tensor_tensor(d1, lg, spread(0), ALU.subtract).then_inc(route_in, 1)
                if kind == "route_top":
                    dve.wait_ge(route_exp, 2 * h + 1)
                    step(nc.vector.tensor_reduce(rs[:, 1, ts], ex, AX_X, ALU.add))
                    step(nc.vector.reciprocal(rs[:, 2, ts], rs[:, 1, ts]))
                    step(nc.vector.tensor_tensor(pr, ex, spread(2), ALU.mult))
                    step(nc.vector.tensor_reduce(rs[:, 3, ts], pr, AX_X, ALU.max))
                    step(nc.vector.tensor_tensor(eq, pr, spread(3), ALU.is_equal))
                    step(nc.vector.tensor_tensor(key, eq, order, ALU.mult))
                    step(nc.vector.tensor_reduce(rs[:, 4, ts], key, AX_X, ALU.max))
                    step(nc.vector.tensor_tensor(oh1, order, spread(4), ALU.is_equal))
                    step(nc.vector.scalar_tensor_tensor(out=p2, in0=oh1, scalar=-2.0, in1=pr, op0=ALU.mult, op1=ALU.add))
                    step(nc.vector.tensor_reduce(rs[:, 5, ts], p2, AX_X, ALU.max))
                    nc.vector.tensor_tensor(rs[:, 6, ts], rs[:, 5, ts], rs[:, 3, ts], ALU.subtract).then_inc(route_in, 1)
                    step(nc.vector.tensor_tensor(eq, p2, spread(5), ALU.is_equal))
                    step(nc.vector.tensor_tensor(key, eq, order, ALU.mult))
                    step(nc.vector.tensor_reduce(rs[:, 8, ts], key, AX_X, ALU.max))
                    step(nc.vector.tensor_tensor(oh2, order, spread(8), ALU.is_equal))
                if kind == "route_weights":
                    dve.wait_ge(route_exp, 2 * h + 2)
                    step(nc.vector.tensor_scalar(rs[:, 9, ts], rs[:, 7, ts], 1.0, None, ALU.add))
                    step(nc.vector.reciprocal(rs[:, 10, ts], rs[:, 9, ts]))
                    step(nc.vector.tensor_scalar(rs[:, 10, ts], rs[:, 10, ts], tg[:, 1:2], None, ALU.mult))
                    step(nc.vector.tensor_tensor(rs[:, 11, ts], rs[:, 10, ts], rs[:, 7, ts], ALU.mult))
                    step(nc.vector.tensor_tensor(oh1, oh1, spread(10), ALU.mult))
                    step(nc.vector.tensor_tensor(oh2, oh2, spread(11), ALU.mult))
                    step(nc.vector.tensor_tensor(cw[:, ts, :], oh1, oh2, ALU.add))

            def misc(kind, b):
                ts = slice(b * TB, (b + 1) * TB)
                if kind == "uT":
                    for j in range(TB):
                        is_full(dve, ("uT", b, j))
                        heads = b_of(("uT", b, j))[:].rearrange("p (h c) -> p h c", c=32)
                        step(nc.vector.reciprocal(rden[:, j, :], heads[:, :, DH]))
                        if b >= 1 and j == 0:
                            is_full(dve, ("cT", b - 1))
                        last = nc.vector.tensor_tensor(cn[:, j], heads[:, :, 0:DH],
                                                       rden[:, j, :].unsqueeze(2).broadcast_to([P, NH, DH]), ALU.mult)
                        last.then_inc(free(("uT", b, j)), 1)
                if kind == "wo":
                    is_full(dve, ("wo", b))
                    yb = y[:, ts, :].rearrange("p t d -> p (t d)")
                    nc.vector.tensor_tensor(yb, b_of(("wo", b))[:, 0:TB * D], yb, ALU.add).then_inc(free(("wo", b)), 1)
                    is_read(dve, ("wo", b))
                    xb = x1[:, ts, :].rearrange("p t d -> p (t d)")
                    step(nc.vector.scalar_tensor_tensor(out=xb, in0=yb, scalar=tg[:, 1:2], in1=xb,
                                                        op0=ALU.mult, op1=ALU.add))
                if kind == "h2":
                    dve.wait_ge(norm3_out, b + 1)
                    for j in range(TB):
                        i = b * TB + j
                        last = nc.vector.tensor_scalar(h2[:, j, :], y[:, i, :], small[:, 11, i:i + 1], None, ALU.mult)
                    last.then_inc(h2_ready, 1)
                if kind == "router":
                    is_full(dve, ("router", b))
                    logits = b_of(("router", b))[:, 0:TB * P].rearrange("p (t e) -> p t e", t=TB)[:, :, 0:NE]
                    nc.vector.tensor_copy(rt[:, 1, ts, :], logits).then_inc(free(("router", b)), 1)
                    if b % 2:
                        routing(kind, b // 2)
                if kind in ("route_top", "route_weights"):
                    routing(kind, b // 2)

            def a_slot(slot):
                n = slot
                if n < NHEADS:
                    is_full(dve, ("max", n))
                    nc.vector.tensor_reduce(mxs[:, n // NH, :, n % NH],
                                            b_of(("max", n))[:].rearrange("p (t s) -> p t s", t=TB),
                                            AX_X, ALU.max).then_inc(free(("max", n)), 1)
                for kind, b in misc_at.get(slot, []):
                    misc(kind, b)

            def accumulate(n):
                e, h = items[n]
                is_full(dve, ("down", n))
                for j in range(4):
                    i = 4 * h + j
                    c = tg[:, 1:2] if e == 0 else cw[:, i, e - 1:e]
                    last = nc.vector.scalar_tensor_tensor(out=x1[:, i, :], in0=b_of(("down", n))[:, j * D:(j + 1) * D],
                                                          scalar=c, in1=x1[:, i, :], op0=ALU.mult, op1=ALU.add)
                last.then_inc(free(("down", n)), 1)

            def m_third(n, k):
                if k < 2:
                    gated, up, out_t = silu[:, n % 2, k, :], ("up", n, k), act_t[:, n % 2, k, :]
                    if n < NEARLY:
                        dve.wait_ge(tanh_ready, 2 * n + k + 1)
                        nc.vector.scalar_tensor_tensor(out=gated, in0=gated, scalar=1.0, in1=b_of(("gate", n, k))[:],
                                                       op0=ALU.add, op1=ALU.mult).then_inc(free(("gate", n, k)), 1)
                    is_read(dve, ("gate", n, k))
                    is_full(dve, up)
                    if n >= 2:
                        is_full(dve, ("down", n - 2))
                    if n < NEARLY:
                        nc.vector.scalar_tensor_tensor(out=out_t, in0=gated, scalar=0.5, in1=b_of(up)[:],
                                                       op0=ALU.mult, op1=ALU.mult).then_inc(free(up), 1)
                    else:
                        nc.vector.tensor_tensor(out_t, gated, b_of(up)[:], ALU.mult).then_inc(free(up), 1)
                elif n >= 1:
                    if n >= 2:
                        is_read(dve, ("down", n - 2))
                    accumulate(n - 1)

            for stage, i in order:
                if stage == "x":
                    x_slot(i)
                elif stage == "a":
                    a_slot(i)
                else:
                    m_third(*thirds[i])

        @block.tensor
        def _(pe):
            def written(use):
                is_read(pe, use)

            def kv(b):
                pe.wait_ge(ld_ctx[min(b, 1)], 16)
                may_fill(pe, ("k", b))
                pe.matmul(b_of(("k", b))[:], Wk_s[0:DC], ctxT[:, b, :], start=True, stop=True).then_inc(full(("k", b)), 1)
                may_fill(pe, ("v", b))
                for c in range(KC):
                    last = pe.matmul(b_of(("v", b))[:, c * D:(c + 1) * D], ctxT[:, b, c * P:(c + 1) * P], Wv_s[0:DC],
                                     start=True, stop=True)
                last.then_inc(full(("v", b)), 1)

            def xn_turn(b):
                pe.wait_ge(xn_ready, b + 1)
                may_fill(pe, ("xnT", b))
                for j in range(TB):
                    last = pe.transpose(b_of(("xnT", b))[:, j * P:(j + 1) * P], y[:, b * TB + j, :], ident[:])
                last.then_inc(full(("xnT", b)), 1)

            def q_proj(b):
                written(("xnT", b))
                may_fill(pe, ("q", b))
                pe.matmul(b_of(("q", b))[:, 0:L], Wq_s, xnT[:, b, :], start=True, stop=True
                          ).then_inc(full(("q", b)), 1)

            pe.wait_ge(ident_ready, 1)
            pe.wait_ge(warm_ready, 1)
            for i in range(WARM):
                pe.matmul(b_of(("k", 0))[:], warm[:, 0:P], warm[:], start=True, stop=True)
            pe.wait_ge(ld_attn, 16)
            kv(0)
            xn_turn(0)
            q_proj(0)

            def x_slot(slot):
                i = slot
                if i < NT:
                    b = i // TB
                    if i % TB == 0:
                        written(("k", b))
                        written(("q", b))
                    may_fill(pe, ("s", i))
                    pe.matmul(b_of(("s", i))[:], qT[:, b, (i % TB) * P:(i % TB + 1) * P], kT[:, b, :],
                              start=True, stop=True).then_inc(full(("s", i)), 1)
                i = slot - 2
                if 0 <= i < NT:
                    written(("pT", i))
                    written(("v", i // TB))
                    may_fill(pe, ("o", i))
                    for c in range(KC):
                        last = pe.matmul(b_of(("o", i))[:, 0:D], probsT[:, i % 2, c, :], vx[:, (i // TB) * KC + c, :],
                                         start=(c == 0), stop=(c == KC - 1))
                    last.then_inc(full(("o", i)), 1)
                b = slot // 2 + 1
                if slot < NT and b < NB:
                    if slot % 2 == 0:
                        kv(b)
                    else:
                        xn_turn(b)
                        q_proj(b)
                i = slot - 1
                if 0 <= i < NT:
                    written(("s", i))
                    may_fill(pe, ("pT", i))
                    for c in range(KC):
                        last = pe.transpose(b_of(("pT", i))[:, c * P:(c + 1) * P], probs[:, i % 2, c * P:(c + 1) * P],
                                            ident[:])
                    last.then_inc(full(("pT", i)), 1)
                if slot >= 5 and slot % 2 == 1 and (slot - 5) // 2 < NB:
                    b = (slot - 5) // 2
                    pe.wait_ge(hs_ready, b + 1)
                    may_fill(pe, ("hT", b))
                    for j in range(TB):
                        last = pe.transpose(b_of(("hT", b))[:, j * P:(j + 1) * P], xs[:, b * TB + j, :], ident[:])
                    last.then_inc(full(("hT", b)), 1)
                if slot >= 6 and slot % 2 == 0 and (slot - 6) // 2 < NB:
                    b = (slot - 6) // 2
                    written(("hT", b))
                    if b == 0:
                        pe.wait_ge(ld_ffn, 16)
                    may_fill(pe, ("qk2", b))
                    for i in range(2):
                        last = pe.matmul(b_of(("qk2", b))[:, i * L:(i + 1) * L], wqk[:, i, :], xnT[:, b, :],
                                         start=True, stop=True)
                    last.then_inc(full(("qk2", b)), 1)
                    may_fill(pe, ("v2", b))
                    for j in range(TB):
                        last = pe.matmul(b_of(("v2", b))[:, j * D:(j + 1) * D], xnT[:, b, j * P:(j + 1) * P], wv_s,
                                         start=True, stop=True)
                    last.then_inc(full(("v2", b)), 1)

            def misc(step, b):
                if step in ("mT0", "mT1"):
                    half = int(step[2])
                    use = ("mT", b, half)
                    is_read(pe, ("max", NH * b + 8 * half + 7))
                    may_fill(pe, use)
                    for j in range(TB):
                        last = pe.transpose(b_of(use)[0:NH // 2, j * P:(j + 1) * P],
                                            mxs[:, b, j, 8 * half:8 * half + 8], ident[:])
                    last.then_inc(full(use), 1)
                if step == "uT":
                    is_read(pe, ("pv", NQ * (b + 1) - 1))
                    for j in range(TB):
                        may_fill(pe, ("uT", b, j))
                        for g in range(NQ):
                            last = pe.transpose(b_of(("uT", b, j))[:, g * P:(g + 1) * P], u[:, g, j * P:(j + 1) * P],
                                                ident[:])
                        last.then_inc(full(("uT", b, j)), 1)
                if step == "cT":
                    for j in range(TB):
                        written(("uT", b, j))
                    may_fill(pe, ("cT", b))
                    for j in range(TB):
                        last = pe.transpose(b_of(("cT", b))[:, j * P:(j + 1) * P], cn[:, j].rearrange("p h d -> p (h d)"),
                                            ident[:])
                    last.then_inc(full(("cT", b)), 1)
                if step == "wo":
                    written(("cT", b))
                    may_fill(pe, ("wo", b))
                    for j in range(TB):
                        last = pe.matmul(b_of(("wo", b))[:, j * D:(j + 1) * D], cT[:, j * P:(j + 1) * P], wo_s,
                                         start=True, stop=True)
                    last.then_inc(full(("wo", b)), 1)
                if step == "h2T":
                    pe.wait_ge(h2_ready, b + 1)
                    may_fill(pe, ("h2T", b))
                    for j in range(TB):
                        last = pe.transpose(b_of(("h2T", b))[:, j * P:(j + 1) * P], h2[:, j, :], ident[:])
                    last.then_inc(full(("h2T", b)), 1)
                if step == "router":
                    is_read(pe, ("h2T", b))
                    if b == 0:
                        pe.wait_ge(router_ready, 1)
                    may_fill(pe, ("router", b))
                    for j in range(TB):
                        last = pe.matmul(b_of(("router", b))[:, j * P:(j + 1) * P], h2T[:, b, j * P:(j + 1) * P],
                                         router_pad[:], start=True, stop=True)
                    last.then_inc(full(("router", b)), 1)


            def a_slot(slot):
                n = slot
                if n < NHEADS:
                    b, h = n // NH, n % NH
                    if h == 0:
                        pe.wait_ge(stacked[b], 128)
                    may_fill(pe, ("max", n))
                    for j in range(TB):
                        last = pe.matmul(b_of(("max", n))[:, j * L:(j + 1) * L],
                                         q_st[:, b % NSTACK, h // 2, j * P:(j + 1) * P],
                                         k_st[:, b % NSTACK, h, :], start=True, stop=True)
                    last.then_inc(full(("max", n)), 1)
                n = slot - LAG
                if 0 <= n < NHEADS:
                    b, h = n // NH, n % NH
                    if h % 8 == 0:
                        pe.wait_ge(m_placed[2 * b + h // 8], 16)
                    may_fill(pe, ("exp", n))
                    for j in range(TB):
                        last = pe.matmul(b_of(("exp", n))[:, j * L:(j + 1) * L],
                                         k_st[:, b % NSTACK, h, j * P:(j + 1) * P],
                                         q_st[:, b % NSTACK, h // 2, :], start=True, stop=True)
                    last.then_inc(full(("exp", n)), 1)
                n = slot - PV_LAG
                if 0 <= n < NHEADS:
                    b, h = n // NH, n % NH
                    is_read(pe, ("exp", n))
                    if h == 0:
                        written(("v2", b))
                    if n % 4 == 0:
                        may_fill(pe, ("pv", n // 4))
                    r = 32 * (n % 4)
                    for j in range(TB):
                        last = pe.matmul(b_of(("pv", n // 4))[r:r + 32, 0:L], vh[:, b * TB + j, h, :], ep[:, n % 3, j, :],
                                         start=(j == 0), stop=(j == TB - 1), tile_position=(0, r))
                    last.then_inc(pv_heads if n % 4 < 3 else full(("pv", n // 4)), 1)
                for step, b in misc_at.get(slot, []):
                    misc(step, b)

            def down_proj(n):
                e, h = items[n]
                is_read(pe, ("up", n, 1))
                may_fill(pe, ("down", n))
                for j in range(4):
                    for f in range(2):
                        last = pe.matmul(b_of(("down", n))[:, j * D:(j + 1) * D], act_t[:, n % 2, f, j * P:(j + 1) * P],
                                         raw[:, e % NRAW, 2, f * D:(f + 1) * D], start=(f == 0), stop=(f == 1))
                last.then_inc(full(("down", n)), 1)

            def m_third(n, k):
                if k == 2:
                    if n >= 1:
                        down_proj(n - 1)
                    return
                e, h = items[n]
                pe.wait_ge(w_split, e + 1)
                pe.wait_ge(h2s_ready, 2 * h + 2)
                hs, fs = slice(h * HALF, (h + 1) * HALF), slice(k * P, (k + 1) * P)
                for i, use in ((0, ("gate", n, k)), (1, ("up", n, k))):
                    may_fill(pe, use)
                    bank = b_of(use)
                    pe.matmul(bank[:], whi[:, e % NSPLIT, i, fs], h2hi[:, hs], start=True, stop=False)
                    pe.matmul(bank[:], whi[:, e % NSPLIT, i, fs], h2lo[:, hs], start=False, stop=False)
                    last = pe.matmul(bank[:], wlo[:, e % NSPLIT, i, fs], h2hi[:, hs], start=False, stop=True)
                    last.then_inc(full(use), 1)

            for stage, i in order:
                if stage == "x":
                    x_slot(i)
                elif stage == "a":
                    a_slot(i)
                else:
                    m_third(*thirds[i])


def kernel(**inputs):
    import numpy as np
    import concourse.bacc as _bacc
    from concourse import mybir as _mybir
    from concourse.bass_utils import run_bass_kernel_spmd as _run

    get = {k.removeprefix("L0_"): np.asarray(v) for k, v in inputs.items()}
    x, context = get["x"], get["ctx_768"]
    NB, L, D = x.shape
    NE = get["ffn_router_w"].shape[1]
    DC, f32 = context.shape[2], x.dtype

    def rows(a):
        return np.broadcast_to(a.reshape(1, -1), (D, a.size))

    def whole(a):
        return np.concatenate([a, np.zeros((D - a.shape[0], a.shape[1]), f32)])

    def by_parity(w):
        return w.reshape(D, 8, 2, 8).transpose(0, 2, 3, 1).reshape(D, D)

    col = lambda a: a.reshape(D, 1)
    attn_w = np.concatenate([whole(get["xattn_Wk"]), whole(get["xattn_Wv"]), get["xattn_Wq"], rows(get["xattn_bv"]),
                             col(get["xattn_bk"]), col(get["xattn_bq"]), rows(get["g_xattn"]), rows(get["g_ffn"])], 1)
    ffn_w = np.concatenate([by_parity(get["ffn_wq"]), by_parity(get["ffn_wk"]), get["ffn_wv"], get["ffn_wo"],
                            get["ffn_router_w"], col(get["ffn_norm1_w"]), col(get["ffn_norm2_w"])], 1)

    def expert(gate, up, down):
        return np.concatenate([gate, up, down.reshape(2, D, D).transpose(1, 0, 2).reshape(D, 2 * D)], 1)

    expert_w = np.stack([expert(get["ffn_sh_gate"], get["ffn_sh_up"], get["ffn_sh_down"])]
                        + [expert(get["ffn_e_gate"][e], get["ffn_e_up"][e], get["ffn_e_down"][e]) for e in range(NE)])
    arrays = {
        "x_tiles": x.reshape(NB * L // D, D, D).transpose(1, 0, 2),
        "ctx_T": context.transpose(2, 0, 1),
        "attn_w": attn_w,
        "ffn_w": ffn_w,
        "expert_w": expert_w,
    }
    arrays = {k: np.ascontiguousarray(a) for k, a in arrays.items()}
    nc = _bacc.Bacc("TRN2", target_bir_lowering=False, num_devices=1)
    args = [nc.dram_tensor(k, a.shape, _mybir.dt.from_np(a.dtype), kind="ExternalInput").ap() for k, a in arrays.items()]
    out = nc.dram_tensor("out_0_dram", arrays["x_tiles"].shape, _mybir.dt.from_np(f32), kind="ExternalOutput").ap()
    flamingo_block(nc, *args, out, NB, L)
    r = _run(nc, [arrays], core_ids=[0])
    return r.results[0]["out_0_dram"].transpose(1, 0, 2).reshape(NB, L, D)
```

```python
from contextlib import ExitStack

import concourse.bass as bass
from concourse import mybir

ALU = mybir.AluOpType
ACT = mybir.ActivationFunctionType
AX_X = mybir.AxisListType.X
F32 = mybir.dt.float32
F32R = mybir.dt.float32r

P = 128
LN_EPS = 1e-5
RMS_EPS = 1e-6
NSTACK = 3
LAG = 13
PV_LAG = LAG + 2
M_STEPS = [("mT0", 8, 8), ("mT1", 17, 17)]
C_STEPS = [("uT0", 31, 31), ("uT1", 32, 32), ("cT", 34, 34), ("wo", 36, 36), ("square", 37, 37), ("h2", 38, 38),
           ("h2T", 41, 41), ("router", 43, 43)]
ROUTE_STEPS = [("route_exp1", 43, 43), ("route_top", 45, 45), ("route_exp2", 45, 45), ("route_weights", 46, 46)]
A_FROM = 10
A_PER_X = 6
M_FROM = 68
M_EVERY = 2
T_FROM = 80
T_EVERY = 2
NEARLY = 4
WARM = 11
NORM_AT = 4
HT_AT = 5
QK_AT = 6
NEP = 6
NRAW = 2
NSPLIT = 4


def bank_uses(pairs):
    place = {}
    for banks, uses in pairs:
        for n, use in enumerate(uses):
            place[use] = (banks[n % len(banks)], n // len(banks))
    return place


def flamingo_block(nc, x_tiles, ctx_T, attn_w, ffn_w, expert_w, out, NB, L):
    D = x_tiles.shape[2]
    KD, _, LK = ctx_T.shape
    DC = KD - 1
    NEXP, _, EW = expert_w.shape
    NE = NEXP - 1
    FF = EW // 3
    NT = NB * L // P
    TB = L // P
    KC = LK // P
    DH = 8
    NH = D // DH
    NG = NH // 2
    NQ = NH // 4
    SCALE_X = float(D) ** -0.5
    SCALE_H = float(DH) ** -0.5
    NHEADS = NB * NH
    HALF = NB * L // 2

    scratch = nc.dram_tensor("split_scratch", [NB, 2, 2, 2, DH, NG, L], F32, kind="Internal").ap()

    SLOTS_X = NT - TB + QK_AT + 1

    def sequence_at(slot, first):
        b, rest = divmod(slot - first, TB)
        return b if rest == 0 and 0 <= b < NB else None

    fill_at, read_at = {}, {}
    for b in range(NB):
        for step, fill, read in M_STEPS + C_STEPS + (ROUTE_STEPS if b % 2 else []):
            fill_at.setdefault(16 * b + fill, []).append((step, b))
            read_at.setdefault(16 * b + read, []).append((step, b))
    SLOTS_A = max(read_at) + 1
    items = [(e, h) for h in range(2) for e in range(NEARLY)] + [(e, h) for e in range(NEARLY, NEXP) for h in range(2)]
    NI = len(items)
    last_item_of = {e: max(n for n, it in enumerate(items) if it[0] == e) for e in range(NEXP)}
    thirds = [(n, k) for n in range(NI) for k in range(3)] + [(NI, 2)]

    order = [("x", i) for i in range(A_FROM)]
    a = 0
    for i in range(A_FROM, SLOTS_X):
        order += [("x", i)] + [("a", a + j) for j in range(A_PER_X)]
        a += A_PER_X
    early = 0
    for i in range(a, SLOTS_A):
        order.append(("a", i))
        due = M_FROM <= i < T_FROM and (i - M_FROM) % M_EVERY == 0 or i >= T_FROM and (i - T_FROM) % T_EVERY == 0
        if due and early < 3 * NEARLY:
            order.append(("m", early))
            early += 1
    order += [("m", i) for i in range(early, len(thirds))]

    pair_uses = {"turn": [("xnT", 0)], "proj": [("fold", 0), ("v", 0), ("q", 0)], "sum": [], "misc": []}
    for stage, i in order:
        if stage == "x":
            if i < NT:
                pair_uses["sum"].append(("s", i))
            if 0 <= i - 2 < NT:
                pair_uses["misc"].append(("o", i - 2))
            b = i // 2 + 1
            if i < NT and b < NB:
                if i % 2 == 0:
                    pair_uses["turn"].append(("xnT", b))
                else:
                    pair_uses["proj"] += [("q", b), ("v", b)]
            if 0 <= i - 1 < NT:
                pair_uses["turn"].append(("pT", i - 1))
            b = sequence_at(i, HT_AT)
            if b is not None:
                pair_uses["turn"].append(("hT", b))
            b = sequence_at(i, QK_AT)
            if b is not None:
                pair_uses["proj"] += [("qk2", b), ("v2", b)]
        if stage == "a":
            if i < NHEADS:
                pair_uses["turn"].append(("max", i))
            if 0 <= i - LAG < NHEADS:
                pair_uses["proj"].append(("exp", i - LAG))
            if 0 <= i - PV_LAG < NHEADS and (i - PV_LAG) % 4 == 3:
                pair_uses["sum"].append(("pv", (i - PV_LAG) // 4))
            for step, b in fill_at.get(i, []):
                if step in ("uT0", "uT1", "mT0", "mT1"):
                    pair_uses["misc"].append((step[:2], b, int(step[2])))
                elif step in ("cT", "wo", "h2T", "router"):
                    pair_uses["misc"].append((step, b))
        if stage == "m":
            n, k = thirds[i]
            if k < 2:
                pair_uses["turn"].append(("gate", n, k))
                pair_uses["proj"].append(("up", n, k))
            elif n >= 1:
                pair_uses["sum"].append(("down", n - 1))
    place = bank_uses([((0, 1), pair_uses["turn"]), ((2, 3), pair_uses["proj"]),
                       ((4, 5), pair_uses["sum"]), ((6, 7), pair_uses["misc"])])

    with ExitStack() as ctx:
        def sb(name, shape, dt=F32):
            return ctx.enter_context(nc.sbuf_tensor(name, shape, dt))

        def sem(name):
            return ctx.enter_context(nc.semaphore(name))

        banks = [ctx.enter_context(nc.psum_tensor(f"bank{i}", [P, 512], F32)) for i in range(8)]
        filled = [sem(f"filled{i}") for i in range(8)]
        emptied = [sem(f"emptied{i}") for i in range(8)]

        ident = sb("ident", [P, P])
        tg = sb("tg", [P, 2])
        attn_s = sb("attn_s", [P, 3 * D + KD + 3])
        WqT_s, Wv_s, bv_row = (attn_s[:, i * D:(i + 1) * D] for i in range(3))
        WkT_s = attn_s[:, 3 * D:3 * D + KD]
        bq_s, gates = attn_s[:, 3 * D + KD:3 * D + KD + 1], attn_s[:, 3 * D + KD + 1:3 * D + KD + 3]
        Wqk_s = sb("Wqk_s", [D, KD])
        bqk_s = sb("bqk_s", [KD, 1])
        ffn_s = sb("ffn_s", [P, 4 * D + NE + 2])
        wqk = ffn_s[:, 0:2 * D].rearrange("k (i m) -> k i m", i=2)
        wv_s, wo_s = ffn_s[:, 2 * D:3 * D], ffn_s[:, 3 * D:4 * D]
        router_s = ffn_s[:, 4 * D:4 * D + NE]
        n1_s, n2_s = ffn_s[:, 4 * D + NE:4 * D + NE + 1], ffn_s[:, 4 * D + NE + 1:4 * D + NE + 2]
        router_pad = sb("router_pad", [D, P])

        xs = sb("xs", [P, NT, D])
        x1 = sb("x1", [P, NT, D])
        y = sb("y", [P, NT, D])
        ctxT = sb("ctxT", [KD, NB, LK])
        vx = sb("vx", [P, NB * KC, D])
        qT = sb("qT", [KD, NB, L])
        xnT = sb("xnT", [D, NB, L])
        probs = sb("probs", [P, 2, LK])
        probsT = sb("probsT", [P, 2, KC, P])
        bn6 = sb("bn6", [P, 2, NT, 6])
        mv = sb("mv", [P, 2, NT, 2])
        small = sb("small", [P, 12, NT])
        neg_half = sb("neg_half", [P, 2, TB])
        ms2 = sb("ms2", [P, NT])
        split = sb("split", [P, 2, 2, 2, L], F32R)
        vh = sb("vh", [P, NT, NH, 32])
        q_st = sb("q_st", [P, NSTACK, NG, L], F32R)
        k_st = sb("k_st", [P, NSTACK, NH, L], F32R)
        mxs = sb("mxs", [P, NB, TB, NH])
        negmT = sb("negmT", [NH // 2, 2, L], F32R)
        ep = sb("ep", [P, NEP, TB, L])
        u = probsT[:].rearrange("p n c t -> p (n c t)").rearrange("p (g s) -> p g s", g=NQ)
        rden = sb("rden", [P, TB, NH])
        cn = sb("cn", [P, TB, NH, DH])
        cT = sb("cT", [D, L])
        h2 = sb("h2", [P, TB, D])
        h2T = probs[:].rearrange("p n s -> p (n s)").rearrange("p (b s) -> p b s", b=NB)
        h2hi, h2lo = sb("h2hi", [D, NB * L], F32R), sb("h2lo", [D, NB * L], F32R)
        rt = sb("rt", [P, 12, NT, NE])
        rs = sb("rs", [P, 12, NT])
        widx = sb("widx", [P, NE])
        cw = sb("cw", [P, NT, NE])
        raw = sb("raw", [P, NRAW, 2, FF])
        down_s = sb("down_s", [P, NSPLIT, FF])
        whi, wlo = sb("whi", [D, NSPLIT, 2, FF], F32R), sb("wlo", [D, NSPLIT, 2, FF], F32R)
        warm = whi[:, 0].rearrange("p k f -> p (k f)")
        silu = sb("silu", [P, 2, 2, HALF])
        act_t = vx[:].rearrange("p a d -> p (a d)").rearrange("p (n f t) -> p n f t", n=2, f=2)

        ld_x = [sem(f"ld_x{i}") for i in range(2)]
        ld_ctx = [sem(f"ld_ctx{i}") for i in range(2)]
        ld_attn, ld_ffn = sem("ld_attn"), sem("ld_ffn")
        ld_raw, ld_down = [sem(f"ld_raw{e}") for e in range(NRAW)], [sem(f"ld_down{e}") for e in range(NSPLIT)]
        pads_copied = sem("pads_copied")
        scratch_written = [sem(f"scratch_written{b}") for b in range(NB)]
        stacked = [sem(f"stacked{b}") for b in range(NB)]
        m_placed = [sem(f"m_placed{i}") for i in range(2 * NB)]
        out_stored = sem("out_stored")
        pool_step, dve_step = sem("pool_step"), sem("dve_step")
        ident_ready, tg_ready, xb_ready = sem("ident_ready"), sem("tg_ready"), sem("xb_ready")
        router_ready, vh_ready, zeros_ready, pick_ready = sem("router_ready"), sem("vh_ready"), sem("zeros_ready"), sem("pick_ready")
        m_rows_zero = sem("m_rows_zero")
        xn_ready, hs_ready, hi_ready = sem("xn_ready"), sem("hs_ready"), sem("hi_ready")
        nb_ready = sem("nb_ready")
        norm1_in, norm1_out, norm2_in, norm2_out, norm3_out = (
            sem("norm1_in"), sem("norm1_out"), sem("norm2_in"), sem("norm2_out"), sem("norm3_out"))
        ms2_ready, h2_ready, h2s_ready, w_split = sem("ms2_ready"), sem("h2_ready"), sem("h2s_ready"), sem("w_split")
        tanh_ready, warm_ready, bqk_ready = sem("tanh_ready"), sem("warm_ready"), sem("bqk_ready")
        route_in, route_exp = sem("route_in"), sem("route_exp")

        def b_of(use):
            return banks[place[use][0]]

        def may_fill(eng, use):
            bank, before = place[use]
            if before:
                eng.wait_ge(emptied[bank], before)

        def full(use):
            return filled[place[use][0]]

        def is_full(eng, use):
            bank, before = place[use]
            eng.wait_ge(filled[bank], before + 1)

        def free(use):
            return emptied[place[use][0]]

        def is_read(eng, use):
            bank, before = place[use]
            eng.wait_ge(emptied[bank], before + 1)

        def k_slot(h):
            return (h % 2) * NG + h // 2

        block = ctx.enter_context(nc.Block())

        def load_expert(sp, e):
            if e >= NRAW:
                sp.wait_ge(w_split, e - NRAW + 1)
            sp.dma_start(raw[:, e % NRAW].rearrange("p k f -> p (k f)"),
                         expert_w[e, :, 0:2 * FF]).then_inc(ld_raw[e % NRAW], 16)
            if e >= NSPLIT:
                is_full(sp, ("down", last_item_of[e - NSPLIT]))
            sp.dma_start(down_s[:, e % NSPLIT], expert_w[e, :, 2 * FF:3 * FF]).then_inc(ld_down[e % NSPLIT], 16)

        def stack(sp, b):
            s = b % NSTACK
            for part in range(2):
                if part == 0:
                    sp.wait_ge(hi_ready, b + 1)
                else:
                    is_read(sp, ("qk2", b))
                for qk in range(2):
                    sp.dma_start(scratch[b, qk, :, part].rearrange("p d g s -> p (d g) s"),
                                 split[:, b % 2, part, qk, :].bitcast(F32)).then_inc(scratch_written[b], 16)
            sp.wait_ge(scratch_written[b], 64)
            if b == 0:
                sp.wait_ge(zeros_ready, 1)
                sp.wait_ge(pick_ready, 2)
            elif b >= NSTACK:
                sp.wait_ge(m_rows_zero, b - NSTACK + 1)
            for p in range(2):
                for a in range(2):
                    r = 32 * p + 16 * a
                    q_src = scratch[b, 0, p, a].rearrange("d g s -> d (g s)").unsqueeze(0).broadcast_to([2, DH, NG * L])
                    sp.dma_start(q_st[r:r + 16, s].rearrange("r g s -> r (g s)").bitcast(F32),
                                 q_src).then_inc(stacked[b], 16)
                k_src = scratch[b, 1, p].rearrange("c d g s -> (c d) (g s)").unsqueeze(0).broadcast_to([2, 2 * DH, NG * L])
                sp.dma_start(k_st[32 * p:32 * p + 32, s, p * NG:(p + 1) * NG].rearrange("r g s -> r (g s)").bitcast(F32),
                             k_src).then_inc(stacked[b], 16)

        def place_m(sp, b, half):
            is_read(sp, ("mT", b, half))
            is_read(sp, ("max", NH * b + 8 * half + 7))
            i, r = 2 * b + half, 64 + 8 * half
            src = negmT[:, i % 2, :].bitcast(F32).unsqueeze(1).broadcast_to([NH // 2, NG // 2, L])
            sp.dma_start(q_st[r:r + 8, b % NSTACK, 4 * half:4 * half + 4, :].bitcast(F32), src).then_inc(m_placed[i], 16)

        @block.sync
        def _(sp):
            sp.dma_start(attn_s[:], attn_w).then_inc(ld_attn, 16)
            sp.dma_start(xs[:, 0:4], x_tiles[:, 0:4]).then_inc(ld_x[0], 16)
            sp.dma_start(ctxT[:, 0:1], ctx_T[:, 0:1]).then_inc(ld_ctx[0], 16)
            sp.dma_start(xs[:, 4:8], x_tiles[:, 4:8]).then_inc(ld_x[1], 16)
            sp.dma_start(ctxT[:, 1:4], ctx_T[:, 1:4]).then_inc(ld_ctx[1], 16)
            sp.dma_start(ffn_s[:], ffn_w).then_inc(ld_ffn, 16)
            for e in range(NRAW):
                load_expert(sp, e)
            sp.wait_ge(zeros_ready, 1)
            sp.wait_ge(pick_ready, 2)
            k_words, q_words = k_st[:].bitcast(F32), q_st[:].bitcast(F32)
            for s in range(1, NSTACK):
                sp.dma_start(k_words[0:32, s, NG:], k_words[0:32, 0, NG:]).then_inc(pads_copied, 16)
                sp.dma_start(k_words[32:64, s, :NG], k_words[32:64, 0, :NG]).then_inc(pads_copied, 16)
                sp.dma_start(k_words[64:P, s], k_words[64:P, 0]).then_inc(pads_copied, 16)
                sp.dma_start(q_words[64:P, s], q_words[64:P, 0]).then_inc(pads_copied, 16)
            sp.wait_ge(pads_copied, 64 * (NSTACK - 1))
            stack(sp, 0)
            stack(sp, 1)
            for e in range(NRAW, NSPLIT):
                load_expert(sp, e)
            place_m(sp, 0, 0)
            stack(sp, 2)
            place_m(sp, 0, 1)
            place_m(sp, 1, 0)
            stack(sp, 3)
            for i in range(3, 8):
                place_m(sp, i // 2, i % 2)
            for e in range(NSPLIT, NEXP):
                load_expert(sp, e)
            for h in range(2):
                is_read(sp, ("down", NI - 2 + h))
                sp.dma_start(out[:, h * 4:h * 4 + 4], x1[:, h * 4:h * 4 + 4]).then_inc(out_stored, 16)
            sp.wait_ge(out_stored, 32)

        @block.gpsimd
        def _(pool):
            done = [0]

            def step(ins):
                done[0] += 1
                ins.then_inc(pool_step, 1)
                pool.wait_ge(pool_step, done[0])

            step(nc.gpsimd.memset(ident[:], 0.0))
            nc.gpsimd.affine_select(out=ident[:], in_=ident[:], compare_op=ALU.not_equal, fill=1.0, base=0,
                                    pattern=[[-1, P]], channel_multiplier=1).then_inc(ident_ready, 1)
            step(nc.gpsimd.memset(neg_half[:], -0.5))
            nc.gpsimd.memset(router_pad[:], 0.0).then_inc(pool_step, 1)
            for i in range(NE):
                last = nc.gpsimd.memset(widx[:, i:i + 1], float(NE - i))
            last.then_inc(pool_step, 1)
            done[0] += 2
            pool.wait_ge(ident_ready, 1)

            k_words = k_st[:, 0].bitcast(F32)
            pool.wait_ge(pool_step, done[0])
            step(nc.gpsimd.memset(k_words[0:32, NG:], 0.0))
            step(nc.gpsimd.memset(k_words[32:64, :NG], 0.0))
            def norm1(b):
                ts = slice(b * TB, (b + 1) * TB)
                pool.wait_ge(norm1_in, b + 1)
                nc.gpsimd.tensor_tensor(small[:, 8, ts], small[:, 0, ts], neg_half[:, 0], ALU.pow).then_inc(norm1_out, 1)

            def norm2(b):
                ts = slice(b * TB, (b + 1) * TB)
                pool.wait_ge(norm2_in, b + 1)
                nc.gpsimd.tensor_tensor(small[:, 5:7, ts], small[:, 3:5, ts], neg_half[:], ALU.pow).then_inc(norm2_out, 1)

            def norm3(b):
                ts = slice(b * TB, (b + 1) * TB)
                pool.wait_ge(ms2_ready, TB * (b + 1))
                step(nc.gpsimd.tensor_scalar(small[:, 7, ts], ms2[:, ts], RMS_EPS, None, ALU.add))
                nc.gpsimd.tensor_tensor(small[:, 11, ts], small[:, 7, ts], neg_half[:, 0], ALU.pow).then_inc(norm3_out, 1)

            norm1(0)
            norm1(1)
            pool.wait_ge(norm1_out, 2)
            nc.gpsimd.memset(q_st[64:P, 0].bitcast(F32), 0.0).then_inc(zeros_ready, 1)
            pool.wait_ge(zeros_ready, 1)
            step(nc.gpsimd.memset(vh[:, 0:4], 0.0))
            norm1(2)
            pool.wait_ge(ld_attn, 16)
            pool.wait_ge(tg_ready, 1)
            step(nc.gpsimd.tensor_scalar(bv_row, bv_row, tg[:, 0:1], None, ALU.mult))

            def add_bias(b):
                pool.wait_ge(ld_x[b // 2], 16)
                pool.wait_ge(xn_ready, b + 1)
                xb = xs[:, b * TB:(b + 1) * TB, :]
                nc.gpsimd.tensor_tensor(xb, xb, bv_row.unsqueeze(1).broadcast_to([P, TB, D]),
                                        ALU.add).then_inc(xb_ready, 1)

            add_bias(0)
            add_bias(1)
            norm1(3)
            step(nc.gpsimd.memset(vh[:, 4:8], 0.0))
            add_bias(2)
            nc.gpsimd.memset(vh[:, :, :, DH:DH + 1], 1.0).then_inc(vh_ready, 1)
            pool.wait_ge(ld_ffn, 16)
            pool.wait_ge(vh_ready, 1)
            nc.gpsimd.tensor_copy(router_pad[:, 0:NE], router_s).then_inc(router_ready, 1)

            def split_weights(e):
                pool.wait_ge(ld_raw[e % NRAW], 16 * (e // NRAW + 1))
                if e >= NSPLIT:
                    is_full(pool, ("up", last_item_of[e - NSPLIT], 1))
                step(nc.gpsimd.tensor_copy(whi[:, e % NSPLIT], raw[:, e % NRAW]))
                nc.gpsimd.tensor_tensor(wlo[:, e % NSPLIT], raw[:, e % NRAW], whi[:, e % NSPLIT].bitcast(F32),
                                        ALU.subtract).then_inc(w_split, 1)

            norm2(0)
            add_bias(3)
            split_weights(0)
            norm2(1)
            split_weights(1)
            norm2(2)
            norm2(3)
            for e in range(2, NSPLIT):
                split_weights(e)

            def split_h2(b):
                is_read(pool, ("h2T", b))
                step(nc.gpsimd.tensor_copy(h2hi[:, b * L:(b + 1) * L], h2T[:, b, :]))
                nc.gpsimd.tensor_tensor(h2lo[:, b * L:(b + 1) * L], h2T[:, b, :],
                                        h2hi[:, b * L:(b + 1) * L].bitcast(F32), ALU.subtract).then_inc(h2s_ready, 1)

            for b in range(NB - NSTACK):
                is_read(pool, ("exp", NH * (b + 1) - 1))
                pool.wait_ge(w_split, NSPLIT)
                nc.gpsimd.memset(q_st[64:96, b % NSTACK].bitcast(F32), 0.0).then_inc(m_rows_zero, 1)
                pool.wait_ge(m_rows_zero, b + 1)
            for b in range(NB):
                norm3(b)
                split_h2(b)
            for e in range(NSPLIT, NEXP):
                split_weights(e)

        @block.scalar
        def _(act):
            act.wait_ge(ident_ready, 1)
            picks = ident[64:P, 64:64 + NH].rearrange("r (g p) -> r p g", p=2)
            for p in range(2):
                nc.scalar.copy(k_st[64:P, 0, p * NG:(p + 1) * NG, :],
                               picks[:, p].unsqueeze(2).broadcast_to([64, NG, L])).then_inc(pick_ready, 1)
            act.wait_ge(ld_attn, 16)
            nc.scalar.activation(tg[:], gates, ACT.Tanh).then_inc(tg_ready, 1)

            is_full(act, ("fold", 0))
            nc.scalar.copy(bqk_s[:], b_of(("fold", 0))[0:KD, P:P + 1]).then_inc(bqk_ready, 1)
            nc.scalar.copy(Wqk_s[:], b_of(("fold", 0))[:, 0:KD]).then_inc(free(("fold", 0)), 1)

            def v_out(b):
                is_full(act, ("v", b))
                nc.scalar.copy(vx[:, b * KC:(b + 1) * KC, :].rearrange("p c d -> p (c d)"),
                               b_of(("v", b))[:]).then_inc(free(("v", b)), 1)

            v_out(0)

            def x_slot(slot):
                i = slot
                if i < NT:
                    act.wait_ge(nb_ready, i + 1)
                    if i >= 2:
                        is_full(act, ("pT", i - 2))
                    nc.scalar.activation(probs[:, i % 2, :], b_of(("s", i))[:], ACT.Exp, bias=small[:, 1, i:i + 1],
                                         scale=SCALE_X, accum_out=small[:, 2, i:i + 1]).then_inc(free(("s", i)), 1)
                    if i % 2 == 1 and i // 2 + 1 < NB:
                        v_out(i // 2 + 1)
                i = slot - 1
                if 0 <= i < NT:
                    is_full(act, ("pT", i))
                    if i >= 2:
                        is_full(act, ("o", i - 2))
                    nc.scalar.copy(probsT[:, i % 2].rearrange("p c t -> p (c t)"),
                                   b_of(("pT", i))[:]).then_inc(free(("pT", i)), 1)
                b = sequence_at(slot, HT_AT)
                if b is not None:
                    is_full(act, ("hT", b))
                    if b == 0:
                        act.wait_ge(ld_ffn, 16)
                    nc.scalar.activation(xnT[:, b, :], b_of(("hT", b))[:, 0:L], ACT.Copy,
                                         scale=n1_s).then_inc(free(("hT", b)), 1)
                b = sequence_at(slot, QK_AT)
                if b is not None:
                    is_full(act, ("qk2", b))
                    if b >= 2:
                        act.wait_ge(scratch_written[b - 2], 64)
                    nc.scalar.copy(split[:, b % 2, 0].rearrange("p q s -> p (q s)"),
                                   b_of(("qk2", b))[:]).then_inc(hi_ready, 1)
                    is_full(act, ("v2", b))
                    if b == 0:
                        act.wait_ge(vh_ready, 1)
                    nc.scalar.copy(vh[:, b * TB:(b + 1) * TB, :, 0:DH],
                                   b_of(("v2", b))[:, 0:TB * D].rearrange("p (t h d) -> p t h d", t=TB, h=NH)
                                   ).then_inc(free(("v2", b)), 1)

            def misc(step, b):
                if step in ("mT0", "mT1"):
                    half = int(step[2])
                    i, use = 2 * b + half, ("mT", b, half)
                    is_full(act, use)
                    if i >= 2:
                        act.wait_ge(m_placed[i - 2], 16)
                    nc.scalar.mul(negmT[:, i % 2, :], b_of(use)[0:NH // 2, 0:L], -1.0).then_inc(free(use), 1)
                if step == "cT":
                    is_full(act, ("cT", b))
                    nc.scalar.copy(cT[:], b_of(("cT", b))[:, 0:L]).then_inc(free(("cT", b)), 1)
                if step == "square":
                    is_read(act, ("wo", b))
                    if b >= 1:
                        is_full(act, ("h2T", b - 1))
                    for j in range(TB):
                        i = b * TB + j
                        last = nc.scalar.activation(h2[:, j, :], y[:, i, :], ACT.Square, scale=float(D) ** -0.5,
                                                    accum_out=ms2[:, i:i + 1])
                        last.then_inc(ms2_ready, 1)
                if step == "h2T":
                    is_full(act, ("h2T", b))
                    nc.scalar.activation(h2T[:, b, :], b_of(("h2T", b))[:, 0:L], ACT.Copy,
                                         scale=n2_s).then_inc(free(("h2T", b)), 1)
                ts = slice(4 * (b // 2), 4 * (b // 2) + 4)
                if step == "route_exp1":
                    act.wait_ge(route_in, 2 * (b // 2) + 1)
                    nc.scalar.activation(rt[:, 3, ts, :], rt[:, 2, ts, :], ACT.Exp).then_inc(route_exp, 1)
                if step == "route_exp2":
                    act.wait_ge(route_in, 2 * (b // 2) + 2)
                    nc.scalar.activation(rs[:, 7, ts], rs[:, 6, ts], ACT.Exp).then_inc(route_exp, 1)

            def a_slot(slot):
                n = slot - LAG
                if 0 <= n < NHEADS:
                    is_full(act, ("exp", n))
                    if n >= NEP:
                        is_full(act, ("pv", (n - NEP) // 4))
                    nc.scalar.activation(ep[:, n % NEP].rearrange("p t s -> p (t s)"), b_of(("exp", n))[:],
                                         ACT.Exp, scale=SCALE_H).then_inc(free(("exp", n)), 1)
                n = slot - PV_LAG - 1
                if 0 <= n < NHEADS and n % 4 == 3:
                    g = n // 4
                    is_full(act, ("pv", g))
                    if g >= NQ:
                        for j in range(TB):
                            is_full(act, ("uT", g // NQ - 1, j))
                    nc.scalar.copy(u[:, g % NQ, :], b_of(("pv", g))[:, 0:L]).then_inc(free(("pv", g)), 1)
                for step, b in read_at.get(slot, []):
                    misc(step, b)

            def m_third(n, k):
                if k == 2:
                    return
                is_full(act, ("gate", n, k))
                if n >= 2:
                    is_read(act, ("up", n - 2, k))
                if n < NEARLY:
                    nc.scalar.activation(silu[:, n % 2, k, :], b_of(("gate", n, k))[:], ACT.Tanh,
                                         scale=0.5).then_inc(tanh_ready, 1)
                else:
                    nc.scalar.activation(silu[:, n % 2, k, :], b_of(("gate", n, k))[:],
                                         ACT.Silu).then_inc(free(("gate", n, k)), 1)

            for stage, i in order:
                if stage == "x":
                    x_slot(i)
                elif stage == "a":
                    a_slot(i)
                else:
                    m_third(*thirds[i])

        @block.vector
        def _(dve):
            done = [0]

            def step(ins):
                done[0] += 1
                ins.then_inc(dve_step, 1)
                dve.wait_ge(dve_step, done[0])

            def norm_stats(k, b, src):
                for i in range(b * TB, (b + 1) * TB):
                    last = nc.vector.bn_stats(bn6[:, k, i, :], src[:, i, :])
                    last.then_inc(dve_step, 1)
                done[0] += TB
                dve.wait_ge(dve_step, done[0])
                for i in range(b * TB, (b + 1) * TB):
                    last = nc.vector.bn_aggr(mv[:, k, i, :], bn6[:, k, i, :])
                    last.then_inc(dve_step, 1)
                done[0] += TB
                dve.wait_ge(dve_step, done[0])

            def first_stats(b):
                dve.wait_ge(ld_x[b // 2], 16)
                norm_stats(0, b, xs)
                ts = slice(b * TB, (b + 1) * TB)
                nc.vector.tensor_scalar(small[:, 0, ts], mv[:, 0, ts, 1], LN_EPS, None, ALU.add).then_inc(norm1_in, 1)

            def first_norm(b):
                dve.wait_ge(norm1_out, b + 1)
                for i in range(b * TB, (b + 1) * TB):
                    last = nc.vector.tensor_scalar(y[:, i, :], xs[:, i, :], mv[:, 0, i, 0:1], small[:, 8, i:i + 1],
                                                   ALU.subtract, ALU.mult)
                last.then_inc(xn_ready, 1)

            def xn_turn(b):
                is_full(dve, ("xnT", b))
                nc.vector.tensor_copy(xnT[:, b, :], b_of(("xnT", b))[:, 0:L]).then_inc(free(("xnT", b)), 1)

            def q_bias(b):
                if b == 0:
                    dve.wait_ge(bqk_ready, 1)
                is_full(dve, ("q", b))
                nc.vector.tensor_scalar(qT[:, b, :], b_of(("q", b))[0:KD, 0:L], bqk_s[:], None,
                                        ALU.add).then_inc(free(("q", b)), 1)

            nc.vector.memset(warm.bitcast(F32), 0.0).then_inc(warm_ready, 1)
            first_stats(0)
            first_norm(0)
            xn_turn(0)
            first_stats(1)
            q_bias(0)
            first_norm(1)

            def second_stats(b):
                ts = slice(b * TB, (b + 1) * TB)
                norm_stats(1, b, x1)
                step(nc.vector.tensor_scalar(small[:, 3, ts], mv[:, 1, ts, 1], LN_EPS, None, ALU.add))
                step(nc.vector.reciprocal(small[:, 0, ts], small[:, 3, ts]))
                step(nc.vector.tensor_tensor(small[:, 4, ts], mv[:, 1, ts, 1], small[:, 0, ts], ALU.mult))
                nc.vector.tensor_scalar(small[:, 4, ts], small[:, 4, ts], RMS_EPS, None, ALU.add).then_inc(norm2_in, 1)

            def second_norm(b):
                dve.wait_ge(norm2_out, b + 1)
                for i in range(b * TB, (b + 1) * TB):
                    last = nc.vector.tensor_scalar(y[:, i, :], x1[:, i, :], mv[:, 1, i, 0:1], small[:, 5, i:i + 1],
                                                   ALU.subtract, ALU.mult)
                    last.then_inc(dve_step, 1)
                done[0] += TB
                dve.wait_ge(dve_step, done[0])
                for i in range(b * TB, (b + 1) * TB):
                    last = nc.vector.tensor_scalar(xs[:, i, :], y[:, i, :], small[:, 6, i:i + 1], None, ALU.mult)
                last.then_inc(hs_ready, 1)

            def x_slot(slot):
                i = slot
                if i < NT:
                    is_full(dve, ("s", i))
                    step(nc.vector.reduce_max(small[:, 7, i:i + 1], b_of(("s", i))[:], AX_X))
                    nc.vector.tensor_scalar(small[:, 1, i:i + 1], small[:, 7, i:i + 1], -SCALE_X, None,
                                            ALU.mult).then_inc(nb_ready, 1)
                    b = i // 2 + 1
                    if i % 2 == 0 and b < NB:
                        xn_turn(b)
                        if b + 1 < NB:
                            first_stats(b + 1)
                    if i % 2 == 1 and b < NB:
                        q_bias(b)
                        if b + 1 < NB:
                            first_norm(b + 1)
                i = slot - 2
                if 0 <= i < NT:
                    is_read(dve, ("s", i))
                    if i == 0:
                        dve.wait_ge(tg_ready, 1)
                    step(nc.vector.reciprocal(small[:, 9, i:i + 1], small[:, 2, i:i + 1]))
                    step(nc.vector.tensor_scalar(small[:, 10, i:i + 1], small[:, 9, i:i + 1], tg[:, 0:1], None, ALU.mult))
                    dve.wait_ge(xb_ready, i // TB + 1)
                    is_full(dve, ("o", i))
                    nc.vector.scalar_tensor_tensor(out=x1[:, i, :], in0=b_of(("o", i))[:, 0:D],
                                                   scalar=small[:, 10, i:i + 1], in1=xs[:, i, :],
                                                   op0=ALU.mult, op1=ALU.add).then_inc(free(("o", i)), 1)
                    if i % TB == TB - 1:
                        for t in range(TB):
                            is_read(dve, ("o", i - t))
                        second_stats(i // TB)
                b = sequence_at(slot, NORM_AT)
                if b is not None:
                    second_norm(b)
                b = sequence_at(slot, QK_AT)
                if b is not None:
                    dve.wait_ge(hi_ready, b + 1)
                    nc.vector.tensor_tensor(split[:, b % 2, 1].rearrange("p q s -> p (q s)"), b_of(("qk2", b))[:],
                                            split[:, b % 2, 0].rearrange("p q s -> p (q s)").bitcast(F32),
                                            ALU.subtract).then_inc(free(("qk2", b)), 1)

            def routing(kind, h):
                ts = slice(4 * h, 4 * h + 4)
                wide = [P, 4, NE]

                def spread(col):
                    return rs[:, col, ts].unsqueeze(2).broadcast_to(wide)

                lg, d1, ex, pr, eq, key, oh1, p2, oh2 = (rt[:, c, ts, :] for c in (1, 2, 3, 4, 5, 6, 7, 8, 9))
                order = widx[:].unsqueeze(1).broadcast_to(wide)
                if kind == "router":
                    is_read(dve, ("router", 2 * h + 1))
                    step(nc.vector.tensor_reduce(rs[:, 0, ts], lg, AX_X, ALU.max))
                    nc.vector.tensor_tensor(d1, lg, spread(0), ALU.subtract).then_inc(route_in, 1)
                if kind == "route_top":
                    dve.wait_ge(route_exp, 2 * h + 1)
                    step(nc.vector.tensor_reduce(rs[:, 1, ts], ex, AX_X, ALU.add))
                    step(nc.vector.reciprocal(rs[:, 2, ts], rs[:, 1, ts]))
                    step(nc.vector.tensor_tensor(pr, ex, spread(2), ALU.mult))
                    step(nc.vector.tensor_reduce(rs[:, 3, ts], pr, AX_X, ALU.max))
                    step(nc.vector.tensor_tensor(eq, pr, spread(3), ALU.is_equal))
                    step(nc.vector.tensor_tensor(key, eq, order, ALU.mult))
                    step(nc.vector.tensor_reduce(rs[:, 4, ts], key, AX_X, ALU.max))
                    step(nc.vector.tensor_tensor(oh1, order, spread(4), ALU.is_equal))
                    step(nc.vector.scalar_tensor_tensor(out=p2, in0=oh1, scalar=-2.0, in1=pr, op0=ALU.mult, op1=ALU.add))
                    step(nc.vector.tensor_reduce(rs[:, 5, ts], p2, AX_X, ALU.max))
                    nc.vector.tensor_tensor(rs[:, 6, ts], rs[:, 5, ts], rs[:, 3, ts], ALU.subtract).then_inc(route_in, 1)
                    step(nc.vector.tensor_tensor(eq, p2, spread(5), ALU.is_equal))
                    step(nc.vector.tensor_tensor(key, eq, order, ALU.mult))
                    step(nc.vector.tensor_reduce(rs[:, 8, ts], key, AX_X, ALU.max))
                    step(nc.vector.tensor_tensor(oh2, order, spread(8), ALU.is_equal))
                if kind == "route_weights":
                    dve.wait_ge(route_exp, 2 * h + 2)
                    step(nc.vector.tensor_scalar(rs[:, 9, ts], rs[:, 7, ts], 1.0, None, ALU.add))
                    step(nc.vector.reciprocal(rs[:, 10, ts], rs[:, 9, ts]))
                    step(nc.vector.tensor_scalar(rs[:, 10, ts], rs[:, 10, ts], tg[:, 1:2], None, ALU.mult))
                    step(nc.vector.tensor_tensor(rs[:, 11, ts], rs[:, 10, ts], rs[:, 7, ts], ALU.mult))
                    step(nc.vector.tensor_tensor(oh1, oh1, spread(10), ALU.mult))
                    step(nc.vector.tensor_tensor(oh2, oh2, spread(11), ALU.mult))
                    step(nc.vector.tensor_tensor(cw[:, ts, :], oh1, oh2, ALU.add))

            def misc(kind, b):
                ts = slice(b * TB, (b + 1) * TB)
                if kind in ("uT0", "uT1"):
                    j = int(kind[2])
                    is_full(dve, ("uT", b, j))
                    heads = b_of(("uT", b, j))[:].rearrange("p (h c) -> p h c", c=32)
                    step(nc.vector.reciprocal(rden[:, j, :], heads[:, :, DH]))
                    if b >= 1 and j == 0:
                        is_full(dve, ("cT", b - 1))
                    nc.vector.tensor_tensor(cn[:, j], heads[:, :, 0:DH],
                                            rden[:, j, :].unsqueeze(2).broadcast_to([P, NH, DH]),
                                            ALU.mult).then_inc(free(("uT", b, j)), 1)
                if kind == "wo":
                    is_full(dve, ("wo", b))
                    yb = y[:, ts, :].rearrange("p t d -> p (t d)")
                    nc.vector.tensor_tensor(yb, b_of(("wo", b))[:, 0:TB * D], yb, ALU.add).then_inc(free(("wo", b)), 1)
                    is_read(dve, ("wo", b))
                    xb = x1[:, ts, :].rearrange("p t d -> p (t d)")
                    step(nc.vector.scalar_tensor_tensor(out=xb, in0=yb, scalar=tg[:, 1:2], in1=xb,
                                                        op0=ALU.mult, op1=ALU.add))
                if kind == "h2":
                    dve.wait_ge(norm3_out, b + 1)
                    for j in range(TB):
                        i = b * TB + j
                        last = nc.vector.tensor_scalar(h2[:, j, :], y[:, i, :], small[:, 11, i:i + 1], None, ALU.mult)
                    last.then_inc(h2_ready, 1)
                if kind == "router":
                    is_full(dve, ("router", b))
                    logits = b_of(("router", b))[:, 0:TB * P].rearrange("p (t e) -> p t e", t=TB)[:, :, 0:NE]
                    nc.vector.tensor_copy(rt[:, 1, ts, :], logits).then_inc(free(("router", b)), 1)
                    if b % 2:
                        routing(kind, b // 2)
                if kind in ("route_top", "route_weights"):
                    routing(kind, b // 2)

            def a_slot(slot):
                n = slot
                if n < NHEADS:
                    is_full(dve, ("max", n))
                    nc.vector.tensor_reduce(mxs[:, n // NH, :, n % NH],
                                            b_of(("max", n))[:].rearrange("p (t s) -> p t s", t=TB),
                                            AX_X, ALU.max).then_inc(free(("max", n)), 1)
                for kind, b in read_at.get(slot, []):
                    misc(kind, b)

            def accumulate(n):
                e, h = items[n]
                is_full(dve, ("down", n))
                for j in range(4):
                    i = 4 * h + j
                    c = tg[:, 1:2] if e == 0 else cw[:, i, e - 1:e]
                    last = nc.vector.scalar_tensor_tensor(out=x1[:, i, :], in0=b_of(("down", n))[:, j * D:(j + 1) * D],
                                                          scalar=c, in1=x1[:, i, :], op0=ALU.mult, op1=ALU.add)
                last.then_inc(free(("down", n)), 1)

            def m_third(n, k):
                if k < 2:
                    gated, up, out_t = silu[:, n % 2, k, :], ("up", n, k), act_t[:, n % 2, k, :]
                    if n < NEARLY:
                        dve.wait_ge(tanh_ready, 2 * n + k + 1)
                        nc.vector.scalar_tensor_tensor(out=gated, in0=gated, scalar=1.0, in1=b_of(("gate", n, k))[:],
                                                       op0=ALU.add, op1=ALU.mult).then_inc(free(("gate", n, k)), 1)
                    is_read(dve, ("gate", n, k))
                    is_full(dve, up)
                    if n >= 2:
                        is_full(dve, ("down", n - 2))
                    if n < NEARLY:
                        nc.vector.scalar_tensor_tensor(out=out_t, in0=gated, scalar=0.5, in1=b_of(up)[:],
                                                       op0=ALU.mult, op1=ALU.mult).then_inc(free(up), 1)
                    else:
                        nc.vector.tensor_tensor(out_t, gated, b_of(up)[:], ALU.mult).then_inc(free(up), 1)
                elif n >= 1:
                    if n >= 2:
                        is_read(dve, ("down", n - 2))
                    accumulate(n - 1)

            for stage, i in order:
                if stage == "x":
                    x_slot(i)
                elif stage == "a":
                    a_slot(i)
                else:
                    m_third(*thirds[i])

        @block.tensor
        def _(pe):
            def written(use):
                is_read(pe, use)

            def v_proj(b):
                pe.wait_ge(ld_ctx[min(b, 1)], 16)
                may_fill(pe, ("v", b))
                for c in range(KC):
                    last = pe.matmul(b_of(("v", b))[:, c * D:(c + 1) * D], ctxT[0:DC, b, c * P:(c + 1) * P], Wv_s[0:DC],
                                     start=True, stop=True)
                last.then_inc(full(("v", b)), 1)

            def xn_turn(b):
                pe.wait_ge(xn_ready, b + 1)
                may_fill(pe, ("xnT", b))
                for j in range(TB):
                    last = pe.transpose(b_of(("xnT", b))[:, j * P:(j + 1) * P], y[:, b * TB + j, :], ident[:])
                last.then_inc(full(("xnT", b)), 1)

            def q_proj(b):
                written(("xnT", b))
                may_fill(pe, ("q", b))
                pe.matmul(b_of(("q", b))[0:KD, 0:L], Wqk_s[:], xnT[:, b, :], start=True, stop=True
                          ).then_inc(full(("q", b)), 1)

            pe.wait_ge(ident_ready, 1)
            pe.wait_ge(warm_ready, 1)
            for i in range(WARM):
                pe.matmul(b_of(("fold", 0))[:], warm[:, 0:P], warm, start=True, stop=True)
            pe.wait_ge(ld_attn, 16)
            pe.matmul(b_of(("fold", 0))[:, 0:KD], WqT_s, WkT_s, start=True, stop=True)
            pe.matmul(b_of(("fold", 0))[0:KD, P:P + 1], WkT_s, bq_s, start=True, stop=True
                      ).then_inc(full(("fold", 0)), 1)
            xn_turn(0)
            written(("fold", 0))
            v_proj(0)
            q_proj(0)

            def x_slot(slot):
                i = slot
                if i < NT:
                    b = i // TB
                    if i % TB == 0:
                        written(("q", b))
                    may_fill(pe, ("s", i))
                    pe.matmul(b_of(("s", i))[:], qT[:, b, (i % TB) * P:(i % TB + 1) * P], ctxT[:, b, :],
                              start=True, stop=True).then_inc(full(("s", i)), 1)
                i = slot - 2
                if 0 <= i < NT:
                    written(("pT", i))
                    written(("v", i // TB))
                    may_fill(pe, ("o", i))
                    for c in range(KC):
                        last = pe.matmul(b_of(("o", i))[:, 0:D], probsT[:, i % 2, c, :], vx[:, (i // TB) * KC + c, :],
                                         start=(c == 0), stop=(c == KC - 1))
                    last.then_inc(full(("o", i)), 1)
                b = slot // 2 + 1
                if slot < NT and b < NB:
                    if slot % 2 == 0:
                        xn_turn(b)
                    else:
                        q_proj(b)
                        v_proj(b)
                i = slot - 1
                if 0 <= i < NT:
                    written(("s", i))
                    may_fill(pe, ("pT", i))
                    for c in range(KC):
                        last = pe.transpose(b_of(("pT", i))[:, c * P:(c + 1) * P], probs[:, i % 2, c * P:(c + 1) * P],
                                            ident[:])
                    last.then_inc(full(("pT", i)), 1)
                b = sequence_at(slot, HT_AT)
                if b is not None:
                    pe.wait_ge(hs_ready, b + 1)
                    may_fill(pe, ("hT", b))
                    for j in range(TB):
                        last = pe.transpose(b_of(("hT", b))[:, j * P:(j + 1) * P], xs[:, b * TB + j, :], ident[:])
                    last.then_inc(full(("hT", b)), 1)
                b = sequence_at(slot, QK_AT)
                if b is not None:
                    written(("hT", b))
                    if b == 0:
                        pe.wait_ge(ld_ffn, 16)
                    may_fill(pe, ("qk2", b))
                    for i in range(2):
                        last = pe.matmul(b_of(("qk2", b))[:, i * L:(i + 1) * L], wqk[:, i, :], xnT[:, b, :],
                                         start=True, stop=True)
                    last.then_inc(full(("qk2", b)), 1)
                    may_fill(pe, ("v2", b))
                    for j in range(TB):
                        last = pe.matmul(b_of(("v2", b))[:, j * D:(j + 1) * D], xnT[:, b, j * P:(j + 1) * P], wv_s,
                                         start=True, stop=True)
                    last.then_inc(full(("v2", b)), 1)

            def misc(step, b):
                if step in ("mT0", "mT1"):
                    half = int(step[2])
                    use = ("mT", b, half)
                    is_read(pe, ("max", NH * b + 8 * half + 7))
                    may_fill(pe, use)
                    for j in range(TB):
                        last = pe.transpose(b_of(use)[0:NH // 2, j * P:(j + 1) * P],
                                            mxs[:, b, j, 8 * half:8 * half + 8], ident[:])
                    last.then_inc(full(use), 1)
                if step in ("uT0", "uT1"):
                    j = int(step[2])
                    is_read(pe, ("pv", NQ * (b + 1) - 1))
                    may_fill(pe, ("uT", b, j))
                    for g in range(NQ):
                        last = pe.transpose(b_of(("uT", b, j))[:, g * P:(g + 1) * P], u[:, g, j * P:(j + 1) * P],
                                            ident[:])
                    last.then_inc(full(("uT", b, j)), 1)
                if step == "cT":
                    for j in range(TB):
                        written(("uT", b, j))
                    may_fill(pe, ("cT", b))
                    for j in range(TB):
                        last = pe.transpose(b_of(("cT", b))[:, j * P:(j + 1) * P], cn[:, j].rearrange("p h d -> p (h d)"),
                                            ident[:])
                    last.then_inc(full(("cT", b)), 1)
                if step == "wo":
                    written(("cT", b))
                    may_fill(pe, ("wo", b))
                    for j in range(TB):
                        last = pe.matmul(b_of(("wo", b))[:, j * D:(j + 1) * D], cT[:, j * P:(j + 1) * P], wo_s,
                                         start=True, stop=True)
                    last.then_inc(full(("wo", b)), 1)
                if step == "h2T":
                    pe.wait_ge(h2_ready, b + 1)
                    may_fill(pe, ("h2T", b))
                    for j in range(TB):
                        last = pe.transpose(b_of(("h2T", b))[:, j * P:(j + 1) * P], h2[:, j, :], ident[:])
                    last.then_inc(full(("h2T", b)), 1)
                if step == "router":
                    is_read(pe, ("h2T", b))
                    if b == 0:
                        pe.wait_ge(router_ready, 1)
                    may_fill(pe, ("router", b))
                    for j in range(TB):
                        last = pe.matmul(b_of(("router", b))[:, j * P:(j + 1) * P], h2T[:, b, j * P:(j + 1) * P],
                                         router_pad[:], start=True, stop=True)
                    last.then_inc(full(("router", b)), 1)


            def a_slot(slot):
                n = slot
                if n < NHEADS:
                    b, h = n // NH, n % NH
                    if h == 0:
                        pe.wait_ge(stacked[b], 96)
                    may_fill(pe, ("max", n))
                    for j in range(TB):
                        last = pe.matmul(b_of(("max", n))[:, j * L:(j + 1) * L],
                                         q_st[:, b % NSTACK, h // 2, j * P:(j + 1) * P],
                                         k_st[:, b % NSTACK, k_slot(h), :], start=True, stop=True)
                    last.then_inc(full(("max", n)), 1)
                n = slot - LAG
                if 0 <= n < NHEADS:
                    b, h = n // NH, n % NH
                    if h % 8 == 0:
                        pe.wait_ge(m_placed[2 * b + h // 8], 16)
                    may_fill(pe, ("exp", n))
                    for j in range(TB):
                        last = pe.matmul(b_of(("exp", n))[:, j * L:(j + 1) * L],
                                         k_st[:, b % NSTACK, k_slot(h), j * P:(j + 1) * P],
                                         q_st[:, b % NSTACK, h // 2, :], start=True, stop=True)
                    last.then_inc(full(("exp", n)), 1)
                n = slot - PV_LAG
                if 0 <= n < NHEADS and n % 4 == 3:
                    b, g = n // NH, n // 4
                    is_read(pe, ("exp", n - 1))
                    is_read(pe, ("exp", n))
                    written(("v2", b))
                    may_fill(pe, ("pv", g))
                    for j in range(TB):
                        for m in range(4 * g, 4 * g + 4):
                            r = 32 * (m % 4)
                            last = pe.matmul(b_of(("pv", g))[r:r + 32, 0:L], vh[:, b * TB + j, m % NH, :],
                                             ep[:, m % NEP, j, :], start=(j == 0), stop=(j == TB - 1),
                                             tile_position=(0, r))
                    last.then_inc(full(("pv", g)), 1)
                for step, b in fill_at.get(slot, []):
                    misc(step, b)

            def down_proj(n):
                e, h = items[n]
                is_read(pe, ("up", n, 1))
                pe.wait_ge(ld_down[e % NSPLIT], 16 * (e // NSPLIT + 1))
                may_fill(pe, ("down", n))
                for j in range(4):
                    for f in range(2):
                        last = pe.matmul(b_of(("down", n))[:, j * D:(j + 1) * D], act_t[:, n % 2, f, j * P:(j + 1) * P],
                                         down_s[:, e % NSPLIT, f * D:(f + 1) * D], start=(f == 0), stop=(f == 1))
                last.then_inc(full(("down", n)), 1)

            def m_third(n, k):
                if k == 2:
                    if n >= 1:
                        down_proj(n - 1)
                    return
                e, h = items[n]
                pe.wait_ge(w_split, e + 1)
                pe.wait_ge(h2s_ready, 2 * h + 2)
                hs, fs = slice(h * HALF, (h + 1) * HALF), slice(k * P, (k + 1) * P)
                for i, use in ((0, ("gate", n, k)), (1, ("up", n, k))):
                    may_fill(pe, use)
                    bank = b_of(use)
                    pe.matmul(bank[:], whi[:, e % NSPLIT, i, fs], h2hi[:, hs], start=True, stop=False)
                    pe.matmul(bank[:], whi[:, e % NSPLIT, i, fs], h2lo[:, hs], start=False, stop=False)
                    last = pe.matmul(bank[:], wlo[:, e % NSPLIT, i, fs], h2hi[:, hs], start=False, stop=True)
                    last.then_inc(full(use), 1)

            for stage, i in order:
                if stage == "x":
                    x_slot(i)
                elif stage == "a":
                    a_slot(i)
                else:
                    m_third(*thirds[i])


def kernel(**inputs):
    import numpy as np
    import concourse.bacc as _bacc
    from concourse import mybir as _mybir
    from concourse.bass_utils import run_bass_kernel_spmd as _run

    get = {k.removeprefix("L0_"): np.asarray(v) for k, v in inputs.items()}
    x, context = get["x"], get["ctx_768"]
    NB, L, D = x.shape
    NE = get["ffn_router_w"].shape[1]
    f32 = x.dtype

    def rows(a):
        return np.broadcast_to(a.reshape(1, -1), (D, a.size))

    def whole(a):
        return np.concatenate([a, np.zeros((D - a.shape[0], a.shape[1]), f32)])

    def by_parity(w):
        return w.reshape(D, 8, 2, 8).transpose(0, 2, 3, 1).reshape(D, D)

    col = lambda a: a.reshape(D, 1)
    attn_w = np.concatenate([get["xattn_Wq"].T, whole(get["xattn_Wv"]), rows(get["xattn_bv"]), get["xattn_Wk"].T,
                             col(get["xattn_bk"]), col(get["xattn_bq"]), rows(get["g_xattn"]), rows(get["g_ffn"])], 1)
    ffn_w = np.concatenate([by_parity(get["ffn_wq"]), by_parity(get["ffn_wk"]), get["ffn_wv"], get["ffn_wo"],
                            get["ffn_router_w"], col(get["ffn_norm1_w"]), col(get["ffn_norm2_w"])], 1)

    def expert(gate, up, down):
        return np.concatenate([gate, up, down.reshape(2, D, D).transpose(1, 0, 2).reshape(D, 2 * D)], 1)

    expert_w = np.stack([expert(get["ffn_sh_gate"], get["ffn_sh_up"], get["ffn_sh_down"])]
                        + [expert(get["ffn_e_gate"][e], get["ffn_e_up"][e], get["ffn_e_down"][e]) for e in range(NE)])
    arrays = {
        "x_tiles": x.reshape(NB * L // D, D, D).transpose(1, 0, 2),
        "ctx_T": np.concatenate([context.transpose(2, 0, 1), np.ones((1,) + context.shape[:2], f32)]),
        "attn_w": attn_w,
        "ffn_w": ffn_w,
        "expert_w": expert_w,
    }
    arrays = {k: np.ascontiguousarray(a) for k, a in arrays.items()}
    nc = _bacc.Bacc("TRN2", target_bir_lowering=False, num_devices=1)
    args = [nc.dram_tensor(k, a.shape, _mybir.dt.from_np(a.dtype), kind="ExternalInput").ap() for k, a in arrays.items()]
    out = nc.dram_tensor("out_0_dram", arrays["x_tiles"].shape, _mybir.dt.from_np(f32), kind="ExternalOutput").ap()
    flamingo_block(nc, *args, out, NB, L)
    r = _run(nc, [arrays], core_ids=[0])
    return r.results[0]["out_0_dram"].transpose(1, 0, 2).reshape(NB, L, D)
```
